# Optimizing a Trainium2 kernel written in Bass

```python
import numpy as np
import jax
import jax.numpy as jnp

def _softmax(x, axis=-1):
    return jax.nn.softmax(x, axis=axis)

def _gelu(x):
    return jax.nn.gelu(x, approximate=True)

def _silu(x):
    return jax.nn.silu(x)

def _sigmoid(x):
    return jax.nn.sigmoid(x)

def _layernorm(x, axis=-1, eps=1e-05):
    m = jnp.mean(x, axis=axis, keepdims=True)
    v = jnp.var(x, axis=axis, keepdims=True)
    return (x - m) / jnp.sqrt(v + eps)

def _scatter_add(tgt, idx, src, axis=0):
    return tgt.at[idx].add(src)

def _segment_sum(src, seg, n):
    return jax.ops.segment_sum(src, seg, n)
kernel_name = 'mk_xattn_ffn_d1_seqx_r4_a1f975'

def setup_inputs(seed: int=0):
    np.random.seed(seed)
    _w = jnp.asarray

    def _rec_inputs():
        import jax
        import jax.numpy as jnp
        _rk = jax.random.key(seed)
        x = 7.22e-05 + 1 * jax.random.normal(jax.random.fold_in(_rk, 1), (4, 512, 512), jnp.float32)
        _lenS = 512 - jax.random.randint(jax.random.fold_in(_rk, 7), (4,), 0, max(1, 512 // 4) + 1, jnp.int32)
        _lenS2 = 512 - jax.random.randint(jax.random.fold_in(_rk, 8), (4,), 0, max(1, 512 // 4) + 1, jnp.int32)
        _ctx_1024P = jax.random.normal(jax.random.fold_in(_rk, 11), (4, 16, 256), jnp.float32)
        _ctx_1024c = jax.random.dirichlet(jax.random.fold_in(_rk, 511), 0.3 * jnp.ones((16,), jnp.float32), (4, 512))
        _ctx_1024t = jnp.einsum('bsk,bkd->bsd', _ctx_1024c, _ctx_1024P)
        _ctx_1024t = _ctx_1024t * jax.lax.rsqrt(jnp.mean(jnp.square(_ctx_1024t)) + 1e-12) * 0.953939
        ctx_1024 = -0.000673644 + 1.00013 * (_ctx_1024t + 0.3 * jax.random.normal(jax.random.fold_in(_rk, 611), (4, 512, 256), jnp.float32))
        return (x, ctx_1024)
    x, ctx_1024 = _rec_inputs()

    def _L0_xattn_setup():
        import jax, jax.numpy as jnp
        import numpy as np
        B, S1, S2, DCA = (2, 512, 256, 16)
        QDIM, KDIM, H = (512, 256, 16)
        HD = QDIM // H
        SCALE = HD ** (-0.5)
        EPS = 1e-06
        DCA_WEIGHT = 1.0

        def _ln(t, w, b):
            m = jnp.mean(t, axis=-1, keepdims=True)
            v = jnp.var(t, axis=-1, keepdims=True)
            return (t - m) * jax.lax.rsqrt(v + EPS) * w + b

        def _attn(q, k, v):
            s = jnp.einsum('bhqd,bhkd->bhqk', q, k) * SCALE
            p = jax.nn.softmax(s, axis=-1)
            return jnp.einsum('bhqk,bhkd->bhqd', p, v)
        key = jax.random.key(seed)
        ks = jax.random.split(key, 8)
        w = lambda k, shape: jax.random.normal(k, shape, jnp.float32) * 0.02
        return {'x': jax.random.normal(ks[0], (B, S1, QDIM), jnp.float32), 'y': jax.random.normal(ks[1], (B, S2 + DCA, KDIM), jnp.float32), 'Wq': w(ks[2], (QDIM, QDIM)), 'bq': jnp.zeros((QDIM,), jnp.float32), 'Wk': w(ks[3], (KDIM, QDIM)), 'bk': jnp.zeros((QDIM,), jnp.float32), 'Wv': w(ks[4], (KDIM, QDIM)), 'bv': jnp.zeros((QDIM,), jnp.float32), 'Wkv_dca': w(ks[5], (KDIM, 2 * QDIM)), 'bkv_dca': jnp.zeros((2 * QDIM,), jnp.float32), 'qn_w': jnp.ones((HD,), jnp.float32), 'qn_b': jnp.zeros((HD,), jnp.float32), 'kn_w': jnp.ones((HD,), jnp.float32), 'kn_b': jnp.zeros((HD,), jnp.float32), 'kn_dca_w': jnp.ones((HD,), jnp.float32), 'kn_dca_b': jnp.zeros((HD,), jnp.float32), 'Wo': w(ks[6], (QDIM, QDIM)), 'bo': jnp.zeros((QDIM,), jnp.float32)}
    _L0_xattn_all = _L0_xattn_setup()
    _L0_xattn_in = {k: v for k, v in _L0_xattn_all.items() if k in ('Wq', 'bq', 'Wk', 'bk', 'Wv', 'bv', 'Wkv_dca', 'bkv_dca', 'qn_w', 'qn_b', 'kn_w', 'kn_b', 'kn_dca_w', 'kn_dca_b', 'Wo', 'bo')}
    del _L0_xattn_all

    def _L0_ffn_setup():
        import jax, jax.numpy as jnp
        import numpy as np
        TOP_K = 6
        CAP_FACTOR = 2

        def _shared_swiglu(x, wg, wu, wd):
            return jax.nn.silu(x @ wg.T) * (x @ wu.T) @ wd.T
        key = jax.random.key(seed)
        ks = jax.random.split(key, 8)
        B, S, D, E, F, FS = (4, 512, 512, 64, 352, 704)
        scale = jnp.float32(0.02)
        return {'hidden_states': jax.random.normal(ks[0], (B, S, D), jnp.float32), 'gate_w': jax.random.normal(ks[1], (E, D), jnp.float32) * scale, 'w_gate': jax.random.normal(ks[2], (E, F, D), jnp.float32) * scale, 'w_up': jax.random.normal(ks[3], (E, F, D), jnp.float32) * scale, 'w_down': jax.random.normal(ks[4], (E, D, F), jnp.float32) * scale, 'sh_gate': jax.random.normal(ks[5], (FS, D), jnp.float32) * scale, 'sh_up': jax.random.normal(ks[6], (FS, D), jnp.float32) * scale, 'sh_down': jax.random.normal(ks[7], (D, FS), jnp.float32) * scale}
    _L0_ffn_all = _L0_ffn_setup()
    _L0_ffn_in = {k: v for k, v in _L0_ffn_all.items() if k in ('gate_w', 'w_gate', 'w_up', 'w_down', 'sh_gate', 'sh_up', 'sh_down')}
    del _L0_ffn_all
    return {'x': x, 'ctx_1024': ctx_1024, 'L0_xattn_Wq': _L0_xattn_in['Wq'], 'L0_xattn_bq': _L0_xattn_in['bq'], 'L0_xattn_Wk': _L0_xattn_in['Wk'], 'L0_xattn_bk': _L0_xattn_in['bk'], 'L0_xattn_Wv': _L0_xattn_in['Wv'], 'L0_xattn_bv': _L0_xattn_in['bv'], 'L0_xattn_Wkv_dca': _L0_xattn_in['Wkv_dca'], 'L0_xattn_bkv_dca': _L0_xattn_in['bkv_dca'], 'L0_xattn_qn_w': _L0_xattn_in['qn_w'], 'L0_xattn_qn_b': _L0_xattn_in['qn_b'], 'L0_xattn_kn_w': _L0_xattn_in['kn_w'], 'L0_xattn_kn_b': _L0_xattn_in['kn_b'], 'L0_xattn_kn_dca_w': _L0_xattn_in['kn_dca_w'], 'L0_xattn_kn_dca_b': _L0_xattn_in['kn_dca_b'], 'L0_xattn_Wo': _L0_xattn_in['Wo'], 'L0_xattn_bo': _L0_xattn_in['bo'], 'L0_ffn_gate_w': _L0_ffn_in['gate_w'], 'L0_ffn_w_gate': _L0_ffn_in['w_gate'], 'L0_ffn_w_up': _L0_ffn_in['w_up'], 'L0_ffn_w_down': _L0_ffn_in['w_down'], 'L0_ffn_sh_gate': _L0_ffn_in['sh_gate'], 'L0_ffn_sh_up': _L0_ffn_in['sh_up'], 'L0_ffn_sh_down': _L0_ffn_in['sh_down']}

def reference(x, ctx_1024, L0_xattn_Wq, L0_xattn_bq, L0_xattn_Wk, L0_xattn_bk, L0_xattn_Wv, L0_xattn_bv, L0_xattn_Wkv_dca, L0_xattn_bkv_dca, L0_xattn_qn_w, L0_xattn_qn_b, L0_xattn_kn_w, L0_xattn_kn_b, L0_xattn_kn_dca_w, L0_xattn_kn_dca_b, L0_xattn_Wo, L0_xattn_bo, L0_ffn_gate_w, L0_ffn_w_gate, L0_ffn_w_up, L0_ffn_w_down, L0_ffn_sh_gate, L0_ffn_sh_up, L0_ffn_sh_down):
    import jax
    import jax.numpy as jnp

    def _L0_xattn_ref(x, y, Wq, bq, Wk, bk, Wv, bv, Wkv_dca, bkv_dca, qn_w, qn_b, kn_w, kn_b, kn_dca_w, kn_dca_b, Wo, bo):
        import jax, jax.numpy as jnp
        import numpy as np
        B, S1, S2, DCA = (2, 512, 256, 16)
        QDIM, KDIM, H = (512, 256, 16)
        HD = QDIM // H
        SCALE = HD ** (-0.5)
        EPS = 1e-06
        DCA_WEIGHT = 1.0

        def _ln(t, w, b):
            m = jnp.mean(t, axis=-1, keepdims=True)
            v = jnp.var(t, axis=-1, keepdims=True)
            return (t - m) * jax.lax.rsqrt(v + EPS) * w + b

        def _attn(q, k, v):
            s = jnp.einsum('bhqd,bhkd->bhqk', q, k) * SCALE
            p = jax.nn.softmax(s, axis=-1)
            return jnp.einsum('bhqk,bhkd->bhqd', p, v)
        b, s1, _ = x.shape
        y_dca = y[:, -DCA:, :]
        y_main = y[:, :-DCA, :]
        kv_dca = (y_dca @ Wkv_dca + bkv_dca).reshape(b, DCA, 2, H, HD)
        k_dca = _ln(kv_dca[:, :, 0], kn_dca_w, kn_dca_b)
        v_dca = kv_dca[:, :, 1]
        s2 = y_main.shape[1]
        q = _ln((x @ Wq + bq).reshape(b, s1, H, HD), qn_w, qn_b)
        kv = jnp.concatenate([y_main @ Wk + bk, y_main @ Wv + bv], axis=-1)
        kv = kv.reshape(b, s2, H, 2 * HD)
        k = _ln(kv[..., :HD], kn_w, kn_b)
        v = kv[..., HD:]
        qT = q.transpose(0, 2, 1, 3)
        ctx = _attn(qT, k.transpose(0, 2, 1, 3), v.transpose(0, 2, 1, 3))
        ctx = ctx.transpose(0, 2, 1, 3).reshape(b, s1, QDIM)
        ctx_dca = _attn(qT, k_dca.transpose(0, 2, 1, 3), v_dca.transpose(0, 2, 1, 3))
        ctx_dca = ctx_dca.transpose(0, 2, 1, 3).reshape(b, s1, QDIM)
        ctx = ctx + DCA_WEIGHT * ctx_dca
        return ctx @ Wo + bo

    def _L0_ffn_ref(hidden_states, gate_w, w_gate, w_up, w_down, sh_gate, sh_up, sh_down):
        import jax, jax.numpy as jnp
        import numpy as np
        TOP_K = 6
        CAP_FACTOR = 2

        def _shared_swiglu(x, wg, wu, wd):
            return jax.nn.silu(x @ wg.T) * (x @ wu.T) @ wd.T
        B, S, D = hidden_states.shape
        E = gate_w.shape[0]
        x = hidden_states.reshape(-1, D)
        N = x.shape[0]
        A = N * TOP_K
        C = CAP_FACTOR * ((A + E - 1) // E)
        scores = jax.nn.softmax(x @ gate_w.T, axis=-1)
        topk_w, topk_idx = jax.lax.top_k(scores, TOP_K)
        topk_w = topk_w / (topk_w.sum(-1, keepdims=True) + 1e-20)
        flat_e = topk_idx.reshape(-1)
        flat_w = topk_w.reshape(-1)
        order = jnp.argsort(flat_e)
        se = flat_e[order]
        st = order // TOP_K
        sw = flat_w[order]
        counts = jnp.bincount(flat_e, length=E)
        offsets = jnp.cumsum(counts) - counts
        pos = jnp.arange(A) - offsets[se]
        valid = pos < C
        pos_c = jnp.minimum(pos, C - 1)
        buf = jnp.zeros((E, C, D), x.dtype).at[se, pos_c].add(jnp.where(valid[:, None], x[st], jnp.zeros((), x.dtype)))
        g = jnp.einsum('ecd,efd->ecf', buf, w_gate)
        u = jnp.einsum('ecd,efd->ecf', buf, w_up)
        eo = jnp.einsum('ecf,edf->ecd', jax.nn.silu(g) * u, w_down)
        gathered = eo[se, pos_c] * (sw * valid.astype(sw.dtype))[:, None]
        y = jnp.zeros_like(x).at[st].add(gathered).reshape(B, S, D)
        return y + _shared_swiglu(hidden_states, sh_gate, sh_up, sh_down)
    x = x + _L0_xattn_ref(_layernorm(x, axis=-1), ctx_1024, L0_xattn_Wq, L0_xattn_bq, L0_xattn_Wk, L0_xattn_bk, L0_xattn_Wv, L0_xattn_bv, L0_xattn_Wkv_dca, L0_xattn_bkv_dca, L0_xattn_qn_w, L0_xattn_qn_b, L0_xattn_kn_w, L0_xattn_kn_b, L0_xattn_kn_dca_w, L0_xattn_kn_dca_b, L0_xattn_Wo, L0_xattn_bo)
    x = x + _L0_ffn_ref(_layernorm(x, axis=-1), L0_ffn_gate_w, L0_ffn_w_gate, L0_ffn_w_up, L0_ffn_w_down, L0_ffn_sh_gate, L0_ffn_sh_up, L0_ffn_sh_down)
    return x

_drawn_inputs = setup_inputs


def setup_inputs(seed=0):
    import zlib

    import numpy as np

    out = dict(_drawn_inputs(seed))
    spreads = {'L0_xattn_bq': (0.0, 0.691),
     'L0_xattn_bk': (0.0, 0.1),
     'L0_xattn_bv': (0.0, 0.1),
     'L0_xattn_bkv_dca': (0.0, 0.1),
     'L0_xattn_qn_w': (1.0, 0.6),
     'L0_xattn_qn_b': (0.0, 0.8),
     'L0_xattn_kn_w': (1.0, 0.6),
     'L0_xattn_kn_b': (0.0, 0.8),
     'L0_xattn_kn_dca_w': (1.0, 0.6),
     'L0_xattn_kn_dca_b': (0.0, 0.8),
     'L0_xattn_bo': (0.0, 0.1)}
    factors = {'L0_ffn_gate_w': 3.404,
     'L0_ffn_w_gate': 3.22,
     'L0_ffn_w_up': 3.164,
     'L0_ffn_w_down': 3.147}
    for name, (base, spread) in spreads.items():
        noise = np.random.default_rng([zlib.crc32(name.encode()), seed]).standard_normal(out[name].shape)
        drawn = base * np.exp(spread * noise) if base else spread * noise
        out[name] = jnp.asarray(drawn.astype(out[name].dtype))
    for name, factor in factors.items():
        out[name] = (out[name] * factor).astype(out[name].dtype)
    return out
```

```python
from contextlib import ExitStack

import concourse.bass as bass
from concourse import mybir

ALU = mybir.AluOpType
ACT = mybir.ActivationFunctionType
F32 = mybir.dt.float32
F32R = mybir.dt.float32r
I32 = mybir.dt.int32
AX = mybir.AxisListType.X

P = 128
NB, S, D = 4, 512, 512
DY = 256
H, HD = 16, 32
DCA = 16
MAIN = S - DCA
T = S // P
DC, YC = D // P, DY // P
E, F, FS, TOPK = 64, 352, 704, 6
N = NB * S
CAP = 2 * ((N * TOPK + E - 1) // E)
CB = CAP // P
NF = 3
FCH = [(0, 128), (128, 128), (256, 96)]
SHARED = FS // F
NO_ROW = float(1 << 20)
SC = HD ** -0.5


class Signal:

    def __init__(self, sem, per, first=0):
        self.sem, self.per, self.first = sem, per, first

    def value(self, turn, n):
        return turn * self.per + (n + self.first)


def bc(ap, shape):
    return ap.broadcast_to(shape)


def attention_phase(nc, ins, out, hbuf, table, kvd, most):
    with ExitStack() as ctx:
        def sb(name, shape, dt=F32):
            return ctx.enter_context(nc.sbuf_tensor(name, shape, dt))

        def sem(name):
            return ctx.enter_context(nc.semaphore(name))

        def sig(name, per, first=0):
            return Signal(sem(name), per, first)

        ps = ctx.enter_context(nc.psum_tensor("ps_a", [P, 8, 512], F32))

        x = sb("x", [P, T, D])
        xh = sb("xh", [P, T, D])
        kt = sb("kt", [P, T, D])
        xT_hi, xT_lo = sb("xT_hi", [P, DC, S], F32R), sb("xT_lo", [P, DC, S], F32R)
        part3 = sb("part3", [P, 2, H, 3 * HD], F32R)
        qs = sb("qs", [P, H, S], F32R)
        ks = sb("ks", [P, H, S], F32R)
        v_main = sb("v_main", [P, T - 1, H, HD + 1])
        v_last = sb("v_last", [P, H, 2, HD + 1])
        prob = sb("prob", [P, 2, T, S])
        nmax = sb("nmax", [P, 2, T, 32], F32R)
        wq_hi, wq_lo = sb("wq_hi", [P, DC, D], F32R), sb("wq_lo", [P, DC, D], F32R)
        wo_hi, wo_lo = sb("wo_hi", [P, DC, D], F32R), sb("wo_lo", [P, DC, D], F32R)
        wk_hi, wk_lo = sb("wk_hi", [P, YC, D], F32R), sb("wk_lo", [P, YC, D], F32R)
        wv_hi, wv_lo = sb("wv_hi", [P, YC, D], F32R), sb("wv_lo", [P, YC, D], F32R)
        wg = sb("wg", [P, DC, E])
        bq, bk, bv, bo = (sb(n, [P, D]) for n in ("bq", "bk", "bv", "bo"))
        lnw = sb("lnw", [P, 6, HD])
        ident = sb("ident", [P, P])
        upper = sb("upper", [P, P])
        ones = sb("ones", [P, P])
        mv = sb("mv", [P, T, 2])
        bst = sb("bst", [P, T, 6])
        std = sb("std", [P, 4])
        rstd = sb("rstd", [P, 4])
        ss = sb("ss", [P, 2, T, H])
        rz = sb("rz", [P, T, 2])
        pv2 = sb("pv2", [P, 2, T, 2, HD])
        eps5, eps6 = sb("eps5", [P, 1]), sb("eps6", [P, 1])
        sums = sb("sums", [P, 64])
        top = sb("top", [P, T, 8])
        carry = sb("carry", [P, T + 1, E])
        e3 = sb("e3", [P, E])
        code8 = sb("code8", [P, T, 8])
        slot = sb("slot", [P, T, 8], I32)
        rows = sb("rows", [P, T, TOPK, 2])
        row_id = sb("row_id", [P, T])
        lm, zs = sb("lm", [P, T]), sb("zs", [P, T])

        cT = kt[:, 0:YC, :]
        cT_hi, cT_lo = (part3[:, :, :, :].rearrange("p a h d -> p (a h d)")[:, i * YC * S:(i + 1) * YC * S]
                        .rearrange("p (c n) -> p c n", c=YC) for i in range(2))
        sq = prob[:, 1, 0:2, :]
        router = prob[:, 1].rearrange("p t n -> p (t n)")
        at = 0
        boards = []
        for width in (E + 2, E + 2, E, E, E, E):
            boards.append(router[:, at:at + T * width].rearrange("p (t e) -> p t e", t=T))
            at += T * width
        sco, rep, mask, wn, code, tmp = boards
        junk = router[:, at:at + E]
        slot_f = router[:, at + E:at + E + T * 8].rearrange("p (t k) -> p t k", t=T)

        stage = prob[:, :, :, :].rearrange("p a t n -> p (a t n)")
        wd_hi = qs[:, 0:4, :].rearrange("p h n -> p (h n)").rearrange("p (c n) -> p c n", c=YC)
        wd_lo = qs[:, 4:8, :].rearrange("p h n -> p (h n)").rearrange("p (c n) -> p c n", c=YC)
        cd = kt[:, 0, 0:YC * NB * DCA].rearrange("p (c n) -> p c n", c=YC)
        bd = kt[:, 1:3, :].rearrange("p t n -> p (t n)")
        cd_hi = qs[:, 8, 0:YC * NB * DCA].rearrange("p (c n) -> p c n", c=YC)
        cd_lo = qs[:, 9, 0:YC * NB * DCA].rearrange("p (c n) -> p c n", c=YC)
        kvd_rows = xh[:, 0:2, :].rearrange("p t n -> p (t n)")

        w1_in, w2_in, small_in, kvd_out, tab_out = (
            sem(n) for n in ("w1_in", "w2_in", "small_in", "kvd_out", "tab_out"))
        consts_done, act_pre, dve_pre, pe_pre = (
            sem(n) for n in ("consts_done", "act_pre", "dve_pre", "pe_pre"))

        def rowvec(v):
            return v.rearrange("(a n) -> a n", a=1)

        ND = NB * DCA
        with nc.Block() as block:
            @block.sync
            def _(sp):
                sp.dma_start(stage[:, 0:DC * D].rearrange("p (c n) -> p c n", c=DC),
                             ins["Wq"].rearrange("(c p) n -> p c n", p=P)).then_inc(w1_in, 16)
                sp.dma_start(stage[:, DC * D:2 * DC * D].rearrange("p (c n) -> p c n", c=DC),
                             ins["Wo"].rearrange("(c p) n -> p c n", p=P)).then_inc(w1_in, 16)
                for dst, v in ((bq, "bq"), (bk, "bk"), (bv, "bv"), (bo, "bo")):
                    sp.dma_start(dst[:], bc(rowvec(ins[v]), [P, D])).then_inc(small_in, 16)
                sp.dma_start(bd, bc(rowvec(ins["bkv_dca"]), [P, 2 * D])).then_inc(small_in, 16)
                for i, v in enumerate(("qn_w", "qn_b", "kn_w", "kn_b", "kn_w", "kn_b")):
                    rows_of = P if i < 4 else P - DCA
                    sp.dma_start(lnw[0:rows_of, i, :], bc(rowvec(ins[v]), [rows_of, HD])).then_inc(small_in, 16)
                for i, v in ((4, "kn_dca_w"), (5, "kn_dca_b")):
                    sp.dma_start(lnw[P - DCA:P, i, :], bc(rowvec(ins[v]), [DCA, HD])).then_inc(small_in, 16)
                sp.dma_start(wg[:], ins["gate_wT"].rearrange("(c p) n -> p c n", p=P)).then_inc(small_in, 16)
                sp.dma_start(cd, ins["ctx_dcaT"].rearrange("(c p) n -> p c n", p=P)).then_inc(small_in, 16)
                sp.wait_ge(dve_pre, 1)
                sp.dma_start(stage[:, 0:YC * D].rearrange("p (c n) -> p c n", c=YC),
                             ins["Wk"].rearrange("(c p) n -> p c n", p=P)).then_inc(w2_in, 16)
                sp.dma_start(stage[:, YC * D:2 * YC * D].rearrange("p (c n) -> p c n", c=YC),
                             ins["Wv"].rearrange("(c p) n -> p c n", p=P)).then_inc(w2_in, 16)
                sp.dma_start(stage[:, 2 * YC * D:4 * YC * D].rearrange("p (c n) -> p c n", c=YC),
                             ins["Wkv_dca"].rearrange("(c p) n -> p c n", p=P)).then_inc(w2_in, 16)
                sp.wait_ge(consts_done, 2)
                sp.dma_start(table.rearrange("(p n) c -> p (n c)", p=P),
                             xh[:, 3, 0:2 * E * CB]).then_inc(tab_out, 16)
                sp.wait_ge(dve_pre, 3)
                sp.dma_start(kvd, kvd_rows[0:ND, :]).then_inc(kvd_out, 16)
                sp.wait_ge(kvd_out, 16)
                sp.wait_ge(tab_out, 16)

            @block.gpsimd
            def _(pool):
                pool.memset(ident[:], 0.0)
                pool.memset(upper[:], 1.0)
                pool.memset(ones[:], 1.0)
                pool.memset(kt[:, 3, :], 0.0)
                pool.memset(xh[:, 3, :], 0.0)
                pool.memset(v_main[:], 1.0)
                pool.memset(v_last[:], 0.0)
                pool.memset(nmax[:].bitcast(F32), 0.0)
                pool.memset(eps5[:], 1e-5)
                pool.memset(eps6[:], 1e-6)
                pool.memset(carry[:], 0.0)
                pool.iota(row_id[:], [[P, T]], base=0, channel_multiplier=1,
                          allow_small_or_imprecise_dtypes=True)
                pool.iota(e3[:], [[CB, E]], base=1, channel_multiplier=0,
                          allow_small_or_imprecise_dtypes=True)
                pool.drain()
                pool.affine_select(out=ident[:], in_=ident[:], compare_op=ALU.not_equal, fill=1.0, base=0,
                                   pattern=[[-1, P]], channel_multiplier=1)
                pool.affine_select(out=upper[:], in_=upper[:], compare_op=ALU.is_gt, fill=0.0, base=0,
                                   pattern=[[1, P]], channel_multiplier=-1)
                pool.affine_select(out=kt[:, 3, 0:MAIN], in_=kt[:, 3, 0:MAIN], compare_op=ALU.not_equal,
                                   fill=1.0, base=-96, pattern=[[0, MAIN]], channel_multiplier=1)
                pool.affine_select(out=kt[:, 3, MAIN:S], in_=kt[:, 3, MAIN:S], compare_op=ALU.not_equal,
                                   fill=1.0, base=-97, pattern=[[0, DCA]], channel_multiplier=1)
                pool.affine_select(out=v_last[:, :, 0, HD:HD + 1], in_=v_last[:, :, 0, HD:HD + 1],
                                   compare_op=ALU.is_ge, fill=1.0, base=-(P - DCA), pattern=[[0, H]],
                                   channel_multiplier=1)
                pool.affine_select(out=v_last[:, :, 1, HD:HD + 1], in_=v_last[:, :, 1, HD:HD + 1],
                                   compare_op=ALU.is_gt, fill=1.0, base=P - DCA, pattern=[[0, H]],
                                   channel_multiplier=-1)
                empty = xh[:, 3, 0:2 * E * CB].rearrange("p (n c) -> p n c", c=2)
                pool.memset(empty[:, :, 0:1], NO_ROW)
                pool.drain().then_inc(consts_done, 2)

            def centre(dve, ap, groups):
                g = ap.rearrange("p (g d) -> p g d", d=HD)
                dve.tensor_reduce(sums[:, 0:groups], g, AX, ALU.add)
                dve.drain()
                dve.tensor_scalar(sums[:, 0:groups], sums[:, 0:groups], 1.0 / HD, None, ALU.mult)
                dve.drain()
                dve.tensor_tensor(g, g, bc(sums[:, 0:groups].unsqueeze(2), [P, groups, HD]), ALU.subtract)
                dve.drain()

            flat = lambda ap: ap.rearrange("p c n -> p (c n)")

            @block.vector
            def _(dve):
                def cut(hi, lo, src):
                    dve.tensor_copy(hi, src)
                    dve.drain()
                    dve.tensor_tensor(lo, src, hi.bitcast(F32), ALU.subtract)

                dve.wait_ge(w1_in, 32)
                centre(dve, stage[:, 0:DC * D], DC * H)
                cut(flat(wq_hi[:]), flat(wq_lo[:]), stage[:, 0:DC * D])
                cut(flat(wo_hi[:]), flat(wo_lo[:]), stage[:, DC * D:2 * DC * D])
                dve.drain().then_inc(dve_pre, 1)
                dve.wait_ge(small_in, 16 * 15)
                centre(dve, bq[:], H)
                centre(dve, bk[:], H)
                centre(dve, bd[:, 0:D], H)
                dve.tensor_scalar(lnw[:, 0:2, :], lnw[:, 0:2, :], SC, None, ALU.mult)
                cut(cd_hi, cd_lo, cd)
                dve.wait_ge(w2_in, 48)
                centre(dve, stage[:, 0:YC * D], YC * H)
                for c in range(YC):
                    o = 2 * YC * D + 2 * D * c
                    centre(dve, stage[:, o:o + D], H)
                cut(flat(wk_hi[:]), flat(wk_lo[:]), stage[:, 0:YC * D])
                cut(flat(wv_hi[:]), flat(wv_lo[:]), stage[:, YC * D:2 * YC * D])
                cut(flat(wd_hi), flat(wd_lo), stage[:, 2 * YC * D:4 * YC * D])
                dve.drain().then_inc(dve_pre, 1)
                dve.wait_ge(pe_pre, 1)
                for c in range(2):
                    dve.tensor_tensor(kvd_rows[0:ND, c * D:(c + 1) * D], ps[0:ND, c, :],
                                      bd[0:ND, c * D:(c + 1) * D], ALU.add)
                dve.drain().then_inc(dve_pre, 1)

            @block.scalar
            def _(act):
                act.wait_ge(consts_done, 2)
                act.wait_ge(pe_pre, 1)
                for h in range(H):
                    act.activation(ks[96:128, h, :], kt[96:128, 3, :], ACT.Copy)
                act.drain().then_inc(act_pre, 1)

            @block.tensor
            def _(pe):
                pe.wait_ge(dve_pre, 2)
                for c in range(2):
                    passes = [(a, w, y) for a, w in ((cd_hi, wd_hi), (cd_hi, wd_lo), (cd_lo, wd_hi))
                              for y in range(YC)]
                    for i, (a, w, y) in enumerate(passes):
                        last = pe.matmul(ps[0:ND, c, :], a[:, y, :], w[:, y, c * D:(c + 1) * D],
                                         start=i == 0, stop=i == len(passes) - 1)
                last.then_inc(pe_pre, 1)

        x_in, ctx_in, kd_in, vd_in, x1_out, h2_out = (
            sig(n, 16) for n in ("x_in", "ctx_in", "kd_in", "vd_in", "x1_out", "h2_out"))
        mean_ready = sig("mean_ready", 2)
        std_ready = sig("std_ready", 2)
        xh_ready = sig("xh_ready", T)
        tr_ready = sig("tr_ready", 3 * DC)
        hi_ready = sig("hi_ready", 3 * DC, first=1)
        lo_ready = sig("lo_ready", 2 * DC)
        ctx_hi, ctx_lo = sig("ctx_hi", 1), sig("ctx_lo", 1, first=1)
        proj_ready = sig("proj_ready", 3 * T)
        qk_raw = sig("qk_raw", 2 * T)
        v_ready = sig("v_ready", T)
        sq_ready = sig("sq_ready", 2 * T)
        ss_ready = sig("ss_ready", 2 * T, first=1)
        hstd_ready = sig("hstd_ready", 2)
        qk_norm = sig("qk_norm", 2 * T)
        qk_done = sig("qk_done", 2 * T, first=1)
        hi3_ready = sig("hi3_ready", 2 * T, first=1)
        lo3_ready = sig("lo3_ready", 2 * T, first=1)
        st_ready = sig("st_ready", 2 * T * 4, first=1)
        st_act = sig("st_act", 2 * T * 2)
        st_dve = sig("st_dve", 2 * T * 2)
        score_ready = sig("score_ready", H)
        nmax_ready = sig("nmax_ready", H)
        nmT_ready = sig("nmT_ready", H)
        nmT_in = sig("nmT_in", H)
        sT_ready = sig("sT_ready", H * T)
        prob_ready = sig("prob_ready", H * T)
        pv_ready = sig("pv_ready", H, first=1)
        pv_taken = sig("pv_taken", H)
        head_done = sig("head_done", H)
        xb_ready = sig("xb_ready", 1)
        att_ready = sig("att_ready", T, first=1)
        x1_ready = sig("x1_ready", T)
        h2_ready = sig("h2_ready", T)
        logit_ready = sig("logit_ready", 1)
        lmax_ready = sig("lmax_ready", 1)
        exp_ready = sig("exp_ready", 1)
        mask_ready = sig("mask_ready", 1)
        pos_ready = sig("pos_ready", 1)
        tab_sent = sig("tab_sent", 1, first=1)
        slot_ready = sig("slot_ready", 1, first=1)
        tab_in = sig("tab_in", 16 * T * TOPK)

        given = dict(vector=(ctx_lo, lo3_ready, ss_ready, slot_ready), gpsimd=(qk_done, tab_sent),
                     tensor=(pv_ready, st_ready, att_ready), scalar=(hi3_ready, hi_ready))
        dve_passed, sp_passed = sem("dve_passed"), sem("sp_passed")
        passed = sem("passed")

        def give_first(eng, name):
            for s in given[name]:
                eng.sem_inc(s.sem, 1)


        HI_LO = lambda a_hi, a_lo, b_hi, b_lo: ((a_hi, b_hi), (a_hi, b_lo), (a_lo, b_hi))
        PROJ, TRB, STB, POB = 4, 6, 4, 7

        with nc.Block() as block:
            @block.sync
            def _(sp):
                with sp.Fori(0, NB) as b:
                    sp.dma_start(x[:], ins["x"][bass.ds(b, 1)].rearrange("a (t p) n -> p (a t) n", p=P)).then_inc(x_in.sem, 16)
                    sp.wait_ge(ctx_lo.sem, ctx_lo.value(b, 0))
                    sp.dma_start(cT, ins["ctxT"][bass.ds(b, 1)].rearrange("a (c p) n -> p (a c) n", p=P)).then_inc(ctx_in.sem, 16)
                    sp.wait_ge(qk_done.sem, qk_done.value(b, 0))
                    sp.dma_start(kt[P - DCA:P, T - 1, :], kvd[bass.ds(b * DCA, DCA), 0:D]).then_inc(kd_in.sem, 16)
                    sp.wait_ge(pv_ready.sem, pv_ready.value(b, 0))
                    sp.dma_start(v_last[P - DCA:P, :, 1, 0:HD],
                                          kvd[bass.ds(b * DCA, DCA), D:2 * D].rearrange("p (h d) -> p h d", d=HD)).then_inc(vd_in.sem, 16)
                    sp.wait_ge(x1_ready.sem, x1_ready.value(b, T))
                    sp.dma_start(out[bass.ds(b, 1)].rearrange("a (t p) n -> p (a t) n", p=P), x[:]).then_inc(x1_out.sem, 16)
                    sp.wait_ge(h2_ready.sem, h2_ready.value(b, T))
                    sp.dma_start(hbuf[bass.ds(b * S, S), :].rearrange("(t p) n -> p t n", p=P), xh[:]).then_inc(h2_out.sem, 16)
                    sp.wait_ge(x1_out.sem, x1_out.value(b, 16))
                    sp.wait_ge(h2_out.sem, h2_out.value(b, 16))
                    sp.sem_inc(sp_passed, 1)

            @block.gpsimd
            def _(pool):
                give_first(pool, "gpsimd")
                with pool.Fori(0, NB) as b:
                    pool.wait_ge(xh_ready.sem, xh_ready.value(b, T))
                    pool.tensor_tensor(x[:], x[:], bc(bo[:].unsqueeze(1), [P, T, D]), ALU.add).then_inc(xb_ready.sem, 1)
                    for u in range(2 * T):
                        pool.wait_ge(qk_norm.sem, qk_norm.value(b, u + 1))
                        t, src = u % T, (xh if u < T else kt)
                        i = 0 if u < T else 2 if t < T - 1 else 4
                        v = src[:, t, :].rearrange("p (h d) -> p h d", d=HD)
                        pool.tensor_tensor(v, v, bc(lnw[:, i, :].unsqueeze(1), [P, H, HD]), ALU.mult)
                        pool.drain()
                        pool.tensor_tensor(v, v, bc(lnw[:, i + 1, :].unsqueeze(1), [P, H, HD]), ALU.add).then_inc(qk_done.sem, 1)
                    for h in range(H):
                        pool.wait_ge(pv_taken.sem, pv_taken.value(b, h + 1))
                        if h == 0:
                            pool.wait_ge(lo3_ready.sem, lo3_ready.value(b, T))
                            pool.wait_ge(hi3_ready.sem, hi3_ready.value(b, T))
                        pool.tensor_tensor(xh[:, :, h * HD:(h + 1) * HD], pv2[:, h % 2, :, 0, :],
                                                        pv2[:, h % 2, :, 1, :], ALU.add).then_inc(head_done.sem, 1)
                    pool.wait_ge(slot_ready.sem, slot_ready.value(b, 1))
                    pool.sem_inc(passed, 1)
                    for t in range(T):
                        for k in range(TOPK):
                            pool.indirect_dma_start(
                                out=table, out_offset=bass.IndirectOffsetOnAxis(slot[:, t, k:k + 1], 0),
                                in_=rows[:, t, k, :], in_offset=None, bounds_check=E * CAP - 1,
                                oob_is_err=False).then_inc(tab_in.sem, 16)
                    pool.wait_ge(tab_in.sem, tab_in.value(b, 16 * T * TOPK))
                    pool.sem_inc(tab_sent.sem, 1)

            def layer_stats(dve, b, ready, order):
                for t in range(T):
                    ready(t)
                    dve.bn_stats(bst[:, t, :], x[:, t, :])
                dve.drain()
                for t in range(T):
                    dve.bn_aggr(mv[:, t, :], bst[:, t, :])
                dve.drain().then_inc(mean_ready.sem, 1)
                dve.wait_ge(std_ready.sem, std_ready.value(b, order + 1))
                dve.reciprocal(rstd[:], std[:])
                dve.drain()

            @block.vector
            def _(dve):
                give_first(dve, "vector")
                with dve.Fori(0, NB) as b:
                    dve.wait_ge(x_in.sem, x_in.value(b, 16))
                    layer_stats(dve, b, lambda t: None, 0)
                    for t in range(T):
                        dve.tensor_scalar(xh[:, t, :], x[:, t, :], mv[:, t, 0:1], rstd[:, t:t + 1],
                                                      ALU.subtract, ALU.mult).then_inc(xh_ready.sem, 1)
                    dve.wait_ge(ctx_hi.sem, ctx_hi.value(b, 1))
                    dve.tensor_tensor(cT_lo[:, :, 0:MAIN], cT[:, :, 0:MAIN], cT_hi[:, :, 0:MAIN].bitcast(F32), ALU.subtract).then_inc(ctx_lo.sem, 1)
                    for c in range(DC):
                        dve.wait_ge(hi_ready.sem, hi_ready.value(b, c + 1))
                        dve.tensor_tensor(xT_lo[:, c, :], ps[:, c, :], xT_hi[:, c, :].bitcast(F32), ALU.subtract).then_inc(lo_ready.sem, 1)
                    for u in range(2 * T):
                        dve.wait_ge(proj_ready.sem, proj_ready.value(b, u + 1))
                        t = u % T
                        m = P - DCA if u == 2 * T - 1 else P
                        dst, bias = (xh, bq) if u < T else (kt, bk)
                        if u == 0:
                            dve.wait_ge(tr_ready.sem, tr_ready.value(b, DC))
                        if u == T:
                            dve.wait_ge(lo3_ready.sem, lo3_ready.value(b, 0))
                            dve.wait_ge(hi3_ready.sem, hi3_ready.value(b, 0))
                        dve.tensor_tensor(dst[0:m, t, :], ps[0:m, PROJ + u % 2, :], bias[0:m, :], ALU.add).then_inc(qk_raw.sem, 1)
                    for half, src in ((0, xh), (1, kt)):
                        for t in range(T):
                            dve.wait_ge(sq_ready.sem, sq_ready.value(b, half * T + t + 1))
                            dve.tensor_reduce(ss[:, half, t, :],
                                                          sq[:, t % 2, :].rearrange("p (h d) -> p h d", d=HD), AX, ALU.add).then_inc(ss_ready.sem, 1)
                        dve.wait_ge(hstd_ready.sem, hstd_ready.value(b, half + 1))
                        dve.reciprocal(ss[:, half], ss[:, half])
                        dve.drain()
                        for t in range(T):
                            v = src[:, t, :].rearrange("p (h d) -> p h d", d=HD)
                            dve.tensor_tensor(v, v, bc(ss[:, half, t, :].unsqueeze(2), [P, H, HD]), ALU.mult).then_inc(qk_norm.sem, 1)
                    for t in range(T):
                        dve.wait_ge(proj_ready.sem, proj_ready.value(b, 2 * T + t + 1))
                        m = P - DCA if t == T - 1 else P
                        dst = v_main[:, t, :, 0:HD] if t < T - 1 else v_last[0:m, :, 0, 0:HD]
                        dve.tensor_tensor(dst, ps[0:m, PROJ + t % 2, :].rearrange("p (h d) -> p h d", d=HD),
                                                     bv[0:m, :].rearrange("p (h d) -> p h d", d=HD), ALU.add).then_inc(v_ready.sem, 1)
                    for u in range(2 * T):
                        src, at = (xh, 2) if u < T else (kt, 1)
                        dve.wait_ge(hi3_ready.sem, hi3_ready.value(b, u + 1))
                        dve.tensor_tensor(part3[:, u % 2, :, at * HD:(at + 1) * HD],
                                                       src[:, u % T, :].rearrange("p (h d) -> p h d", d=HD),
                                                       part3[:, u % 2, :, 0:HD].bitcast(F32), ALU.subtract).then_inc(lo3_ready.sem, 1)
                        for g in (1, 3):
                            dve.wait_ge(st_ready.sem, st_ready.value(b, 4 * u + g + 1))
                            dst = (qs if u < T else ks)[0:96, 4 * g:4 * g + 4, (u % T) * P:(u % T + 1) * P]
                            dve.tensor_copy(dst, ps[0:96, g, :].rearrange("p (h n) -> p h n", n=P)).then_inc(st_dve.sem, 1)
                    for h in range(H + 1):
                        if h < H:
                            dve.wait_ge(score_ready.sem, score_ready.value(b, h + 1))
                            if h >= 2:
                                dve.wait_ge(nmT_ready.sem, nmT_ready.value(b, h - 1))
                            dve.tensor_reduce(nmax[:, h % 2, :, 0], ps[:, 0:T, 0:MAIN], AX, ALU.max, negate=True)
                            dve.tensor_reduce(nmax[:, h % 2, :, 1], ps[:, 0:T, MAIN:S], AX, ALU.max, negate=True)
                            dve.drain().then_inc(nmax_ready.sem, 1)
                        if h >= 1:
                            g = h - 1
                            dve.wait_ge(pv_ready.sem, pv_ready.value(b, g + 1))
                            pv = ps[:, POB, 0:T * 2 * (HD + 1)].rearrange("p (t c d) -> p t c d", t=T, c=2)
                            if g >= 2:
                                dve.wait_ge(head_done.sem, head_done.value(b, g - 1))
                            dve.reciprocal(rz[:], pv[:, :, :, HD])
                            dve.drain()
                            dve.tensor_tensor(pv2[:, g % 2], pv[:, :, :, 0:HD],
                                                          bc(rz[:].unsqueeze(3), [P, T, 2, HD]), ALU.mult).then_inc(pv_taken.sem, 1)
                    for c in range(DC):
                        dve.wait_ge(hi_ready.sem, hi_ready.value(b, DC + c + 1))
                        dve.tensor_tensor(xT_lo[:, c, :], ps[:, c, :], xT_hi[:, c, :].bitcast(F32), ALU.subtract).then_inc(lo_ready.sem, 1)
                    dve.wait_ge(xb_ready.sem, xb_ready.value(b, 1))

                    def residual(t):
                        dve.wait_ge(att_ready.sem, att_ready.value(b, t + 1))
                        dve.tensor_tensor(x[:, t, :], ps[:, PROJ + t % 2, :], x[:, t, :], ALU.add).then_inc(x1_ready.sem, 1)
                        dve.drain()

                    layer_stats(dve, b, residual, 1)
                    for t in range(T):
                        dve.tensor_scalar(xh[:, t, :], x[:, t, :], mv[:, t, 0:1], rstd[:, t:t + 1],
                                                      ALU.subtract, ALU.mult).then_inc(h2_ready.sem, 1)
                    dve.wait_ge(logit_ready.sem, logit_ready.value(b, 1))
                    logits = ps[:, 5, 0:T * E].rearrange("p (t e) -> p t e", e=E)
                    dve.tensor_reduce(lm[:], logits, AX, ALU.max, negate=True)
                    dve.drain().then_inc(lmax_ready.sem, 1)
                    dve.wait_ge(exp_ready.sem, exp_ready.value(b, 1))
                    dve.memset(sco[:, :, E:E + 1], -1.0)
                    dve.memset(sco[:, :, E + 1:E + 2], -2.0)
                    dve.reciprocal(zs[:], zs[:])
                    dve.drain()
                    probs = sco[:, :, 0:E]
                    dve.tensor_tensor(probs, probs, bc(zs[:].unsqueeze(2), [P, T, E]), ALU.mult)
                    dve.drain()
                    for t in range(T):
                        dve.max(top[:, t, :], sco[:, t, 0:E])
                    dve.drain()
                    dve.tensor_reduce(lm[:], top[:, :, 0:TOPK], AX, ALU.add)
                    dve.memset(top[:, :, 6:7], -1.0)
                    dve.memset(top[:, :, 7:8], -2.0)
                    dve.drain()
                    dve.tensor_scalar(lm[:], lm[:], 1e-20, None, ALU.add)
                    for t in range(T):
                        dve.match_replace(rep[:, t, :], top[:, t, :], sco[:, t, :], -3.0)
                    dve.drain()
                    dve.reciprocal(lm[:], lm[:])
                    dve.tensor_scalar(mask, rep[:, :, 0:E], -2.5, None, ALU.is_lt)
                    dve.tensor_copy(carry[:, 0, :], carry[:, T, :])
                    dve.drain()
                    for t in range(T):
                        dve.tensor_tensor(carry[:, t + 1, :], carry[:, t, :], mask[:, t, :], ALU.add)
                        dve.drain()
                    dve.tensor_tensor(wn[:], probs, bc(lm[:].unsqueeze(2), [P, T, E]), ALU.mult).then_inc(mask_ready.sem, 1)
                    dve.wait_ge(pos_ready.sem, pos_ready.value(b, 1))
                    pos = ps[:, 5, 0:T * E].rearrange("p (t e) -> p t e", e=E)
                    dve.tensor_scalar(code, pos, float(E * CB), None, ALU.mult)
                    dve.tensor_scalar(tmp, pos, float(P) - 0.5, -float(P * E * CB - 1), ALU.is_gt, ALU.mult)
                    dve.drain()
                    dve.tensor_tensor(code, code, tmp, ALU.add)
                    dve.drain()
                    dve.tensor_scalar(tmp, pos, 2.0 * P - 0.5, -float(P * E * CB - 1), ALU.is_gt, ALU.mult)
                    dve.drain()
                    dve.tensor_tensor(code, code, tmp, ALU.add)
                    dve.drain()
                    dve.tensor_tensor(code, code, bc(e3[:].unsqueeze(1), [P, T, E]), ALU.add)
                    dve.tensor_scalar(tmp, pos, float(CAP) - 0.5, None, ALU.is_lt)
                    dve.drain()
                    dve.tensor_tensor(tmp, tmp, mask, ALU.mult)
                    dve.drain()
                    dve.wait_ge(tab_sent.sem, tab_sent.value(b, 0))
                    dve.tensor_tensor(code, code, tmp, ALU.mult)
                    dve.drain()
                    for t in range(T):
                        dve.max(code8[:, t, :], code[:, t, :])
                    dve.drain()
                    dve.tensor_scalar(slot_f, code8[:], 0.5, NO_ROW, ALU.is_lt, ALU.mult)
                    dve.tensor_copy(rows[:, :, :, 0], bc(row_id[:].unsqueeze(2), [P, T, TOPK]))
                    for t in range(T):
                        for k in range(TOPK):
                            dve.scalar_tensor_tensor(junk, code[:, t, :], code8[:, t, k:k + 1], wn[:, t, :],
                                                     ALU.is_equal, ALU.mult, accum_out=rows[:, t, k, 1:2])
                            dve.drain()
                    dve.tensor_tensor(slot_f, slot_f, code8[:], ALU.add)
                    dve.tensor_scalar(row_id[:], row_id[:], float(S), None, ALU.add)
                    dve.drain()
                    dve.tensor_scalar(slot[:], slot_f, -1.0, None, ALU.add)
                    dve.drain().then_inc(slot_ready.sem, 1)
                    dve.wait_ge(h2_out.sem, h2_out.value(b, 16))
                    dve.sem_inc(dve_passed, 1)

            def take(act, b, u):
                for g in (0, 2):
                    act.wait_ge(st_ready.sem, st_ready.value(b, 4 * u + g + 1))
                    dst = (qs if u < T else ks)[0:96, 4 * g:4 * g + 4, (u % T) * P:(u % T + 1) * P]
                    act.activation(dst, ps[0:96, g, :].rearrange("p (h n) -> p h n", n=P), ACT.Copy).then_inc(st_act.sem, 1)

            @block.scalar
            def _(act):
                give_first(act, "scalar")
                with act.Fori(0, NB) as b:
                    act.wait_ge(mean_ready.sem, mean_ready.value(b, 1))
                    act.activation(std[:], mv[:, :, 1], ACT.Sqrt, bias=eps5[:]).then_inc(std_ready.sem, 1)
                    act.wait_ge(ctx_in.sem, ctx_in.value(b, 16))
                    act.wait_ge(st_ready.sem, st_ready.value(b, 0))
                    act.activation(cT_hi[:, :, 0:MAIN], cT[:, :, 0:MAIN], ACT.Copy).then_inc(ctx_hi.sem, 1)
                    for c in range(DC):
                        act.wait_ge(tr_ready.sem, tr_ready.value(b, c + 1))
                        act.wait_ge(att_ready.sem, att_ready.value(b, 0))
                        act.activation(xT_hi[:, c, :], ps[:, c, :], ACT.Copy).then_inc(hi_ready.sem, 1)
                    act.wait_ge(kd_in.sem, kd_in.value(b, 16))
                    for half, src in ((0, xh), (1, kt)):
                        for t in range(T):
                            u = half * T + t
                            act.wait_ge(qk_raw.sem, qk_raw.value(b, u + 1))
                            if u >= 2:
                                act.wait_ge(ss_ready.sem, ss_ready.value(b, u - 1))
                            else:
                                act.wait_ge(ss_ready.sem, ss_ready.value(b, 0))
                            act.activation(sq[:, t % 2, :], src[:, t, :], ACT.Square).then_inc(sq_ready.sem, 1)
                        act.wait_ge(ss_ready.sem, ss_ready.value(b, (half + 1) * T))
                        act.activation(ss[:, half], ss[:, half], ACT.Sqrt, bias=eps6[:], scale=1.0 / HD).then_inc(hstd_ready.sem, 1)
                    for u in range(2 * T):
                        src = xh if u < T else kt
                        act.wait_ge(qk_done.sem, qk_done.value(b, u + 1))
                        if u == 0:
                            act.wait_ge(proj_ready.sem, proj_ready.value(b, 3 * T))
                        if u >= 2:
                            act.wait_ge(st_ready.sem, st_ready.value(b, 4 * (u - 1)))
                        v = src[:, u % T, :].rearrange("p (h d) -> p h d", d=HD)
                        other = 1 if u < T else 2
                        act.activation(part3[:, u % 2, :, 0:HD], v, ACT.Copy)
                        act.activation(part3[:, u % 2, :, other * HD:(other + 1) * HD], v, ACT.Copy).then_inc(hi3_ready.sem, 1)
                        if u >= 1:
                            take(act, b, u - 1)
                    take(act, b, 2 * T - 1)
                    for h in range(H):
                        act.wait_ge(nmT_ready.sem, nmT_ready.value(b, h + 1))
                        act.activation(qs[96:128, h, :], ps[0:32, TRB, :], ACT.Copy).then_inc(nmT_in.sem, 1)
                        for c in range(T):
                            act.wait_ge(sT_ready.sem, sT_ready.value(b, h * T + c + 1))
                            if h >= 2 and c == 0:
                                act.wait_ge(pv_ready.sem, pv_ready.value(b, h - 1))
                            act.activation(prob[:, h % 2, c, :], ps[:, STB + c % 2, :], ACT.Exp).then_inc(prob_ready.sem, 1)
                    for c in range(DC):
                        act.wait_ge(tr_ready.sem, tr_ready.value(b, DC + c + 1))
                        act.activation(xT_hi[:, c, :], ps[:, c, :], ACT.Copy).then_inc(hi_ready.sem, 1)
                    act.wait_ge(mean_ready.sem, mean_ready.value(b, 2))
                    act.activation(std[:], mv[:, :, 1], ACT.Sqrt, bias=eps5[:]).then_inc(std_ready.sem, 1)
                    for c in range(DC):
                        act.wait_ge(tr_ready.sem, tr_ready.value(b, 2 * DC + c + 1))
                        act.activation(prob[:, 0, c, :], ps[:, c, :], ACT.Copy).then_inc(hi_ready.sem, 1)
                    act.wait_ge(lmax_ready.sem, lmax_ready.value(b, 1))
                    for t in range(T):
                        act.activation(sco[:, t, 0:E], ps[:, 5, t * E:(t + 1) * E], ACT.Exp,
                                       bias=lm[:, t:t + 1], accum_out=zs[:, t:t + 1])
                    act.drain().then_inc(exp_ready.sem, 1)

            @block.tensor
            def _(pe):
                def transpose_rows(b, ready, of, base):
                    for c in range(DC):
                        for t in range(T):
                            if c == 0:
                                ready(t)
                            last = pe.transpose(ps[:, c, t * P:(t + 1) * P], of[:, t, c * P:(c + 1) * P], ident[:])
                        last.then_inc(tr_ready.sem, 1)

                def product(dst, m, t, pairs, chunks, done):
                    steps = [(l, r, c) for l, r in pairs for c in range(chunks)]
                    for i, (l, r, c) in enumerate(steps):
                        last = pe.matmul(dst, l[:, c, t * P:t * P + m], r[:, c, :],
                                         start=i == 0, stop=i == len(steps) - 1)
                    last.then_inc(done.sem, 1)

                give_first(pe, "tensor")
                with pe.Fori(0, NB) as b:
                    pe.wait_ge(hi_ready.sem, hi_ready.value(b, 0))
                    transpose_rows(b, lambda t: pe.wait_ge(xh_ready.sem, xh_ready.value(b, t + 1)), xh, 0)
                    pos_free = slot_ready
                    pe.wait_ge(pos_free.sem, pos_free.value(b, 0))
                    for u in range(3 * T):
                        t = u % T
                        m = P - DCA if u >= T and t == T - 1 else P
                        if u == 0:
                            pe.wait_ge(lo_ready.sem, lo_ready.value(b, DC))
                        if u == T:
                            pe.wait_ge(ctx_lo.sem, ctx_lo.value(b, 1))
                        if 2 <= u:
                            if u - 2 < 2 * T:
                                pe.wait_ge(qk_raw.sem, qk_raw.value(b, u - 1))
                            else:
                                pe.wait_ge(v_ready.sem, v_ready.value(b, u - 1 - 2 * T))
                        dst = ps[0:m, PROJ + u % 2, :]
                        if u < T:
                            product(dst, m, t, HI_LO(xT_hi, xT_lo, wq_hi, wq_lo), DC, proj_ready)
                        elif u < 2 * T:
                            product(dst, m, t, HI_LO(cT_hi, cT_lo, wk_hi, wk_lo), YC, proj_ready)
                        else:
                            product(dst, m, t, HI_LO(cT_hi, cT_lo, wv_hi, wv_lo), YC, proj_ready)
                    for u in range(2 * T):
                        pe.wait_ge(lo3_ready.sem, lo3_ready.value(b, u + 1))
                        for g in range(4):
                            if u == 0 and g == 0:
                                pe.wait_ge(lo_ready.sem, lo_ready.value(b, DC))
                            if u >= 1:
                                if g % 2:
                                    pe.wait_ge(st_dve.sem, st_dve.value(b, 2 * (u - 1) + g // 2 + 1))
                                else:
                                    pe.wait_ge(st_act.sem, st_act.value(b, 2 * (u - 1) + g // 2 + 1))
                            for i in range(4):
                                h = 4 * g + i
                                last = pe.transpose(ps[0:96, g, i * P:(i + 1) * P], part3[:, u % 2, h, :].bitcast(F32), ident[:])
                            last.then_inc(st_ready.sem, 1)
                    pe.wait_ge(st_act.sem, st_act.value(b, 4 * T))
                    pe.wait_ge(st_dve.sem, st_dve.value(b, 4 * T))
                    pe.wait_ge(v_ready.sem, v_ready.value(b, T))
                    pe.wait_ge(vd_in.sem, vd_in.value(b, 16))

                    def scores(h):
                        for t in range(T):
                            last = pe.matmul(ps[:, t, :], qs[0:96, h, t * P:(t + 1) * P], ks[0:96, h, :], start=True, stop=True)
                        last.then_inc(score_ready.sem, 1)

                    def weigh(h, t):
                        prow = prob[:, h % 2, :, t * P:(t + 1) * P]
                        o = t * 2 * (HD + 1)
                        pe.matmul(ps[:, POB, o:o + 2 * (HD + 1)], prow[:, T - 1, :],
                                  v_last[:, h].rearrange("p c d -> p (c d)"), start=True, stop=False)
                        for c in range(T - 1):
                            last = pe.matmul(ps[:, POB, o:o + HD + 1], prow[:, c, :], v_main[:, c, h, :],
                                             start=False, stop=c == T - 2)
                        return last

                    scores(0)
                    for h in range(H + 1):
                        if h < H:
                            pe.wait_ge(nmax_ready.sem, nmax_ready.value(b, h + 1))
                            if h >= 1:
                                pe.wait_ge(nmT_in.sem, nmT_in.value(b, h))
                            for t in range(T):
                                last = pe.transpose(ps[0:32, TRB, t * P:(t + 1) * P], nmax[:, h % 2, t, :].bitcast(F32), ident[:])
                            last.then_inc(nmT_ready.sem, 1)
                            if h + 1 < H:
                                scores(h + 1)
                            pe.wait_ge(nmT_in.sem, nmT_in.value(b, h + 1))
                        if h >= 1:
                            pe.wait_ge(prob_ready.sem, prob_ready.value(b, h * T))
                            if h >= 2:
                                pe.wait_ge(pv_taken.sem, pv_taken.value(b, h - 1))
                        for c in range(T):
                            if h < H:
                                if h * T + c >= 2:
                                    pe.wait_ge(prob_ready.sem, prob_ready.value(b, h * T + c - 1))
                                pe.matmul(ps[:, STB + c % 2, :], ks[:, h, c * P:(c + 1) * P], qs[:, h, :], start=True, stop=True).then_inc(sT_ready.sem, 1)
                            if h >= 1:
                                last = weigh(h - 1, c)
                        if h >= 1:
                            last.then_inc(pv_ready.sem, 1)
                    transpose_rows(b, lambda t: pe.wait_ge(head_done.sem, head_done.value(b, H)), xh, DC)
                    for t in range(T):
                        if t == 0:
                            pe.wait_ge(lo_ready.sem, lo_ready.value(b, 2 * DC))
                        if t >= 2:
                            pe.wait_ge(x1_ready.sem, x1_ready.value(b, t - 1))
                        product(ps[:, PROJ + t % 2, :], P, t, HI_LO(xT_hi, xT_lo, wo_hi, wo_lo), DC, att_ready)
                    transpose_rows(b, lambda t: pe.wait_ge(h2_ready.sem, h2_ready.value(b, t + 1)), xh, 2 * DC)
                    pe.wait_ge(hi_ready.sem, hi_ready.value(b, 3 * DC))
                    pe.wait_ge(x1_ready.sem, x1_ready.value(b, T))
                    for t in range(T):
                        for c in range(DC):
                            last = pe.matmul(ps[:, 5, t * E:(t + 1) * E], prob[:, 0, c, t * P:(t + 1) * P], wg[:, c, :],
                                             start=c == 0, stop=c == DC - 1)
                    last.then_inc(logit_ready.sem, 1)
                    pe.wait_ge(mask_ready.sem, mask_ready.value(b, 1))
                    for t in range(T):
                        pe.matmul(ps[:, 5, t * E:(t + 1) * E], upper[:], mask[:, t, :], start=True, stop=False)
                        last = pe.matmul(ps[:, 5, t * E:(t + 1) * E], ones[:], carry[:, t, :], start=False, stop=True)
                    last.then_inc(pos_ready.sem, 1)

        counted, most_f = sem("counted"), lm
        with nc.Block() as block:
            @block.tensor
            def _(pe):
                pe.matmul(ps[:, 0, 0:E], ones[:], carry[:, T, :], start=True, stop=True).then_inc(counted, 1)

            @block.vector
            def _(dve):
                dve.wait_ge(counted, 1)
                dve.tensor_reduce(most_f[:, 0:1], ps[:, 0, 0:E], AX, ALU.max)
                dve.drain()
                dve.tensor_copy(most[:], most_f[:, 0:1])



class Item:

    def __init__(self, pair, q, items):
        self.pair, self.q, self.items = pair, q, items

    def __add__(self, n):
        return Item(self.pair, self.q + n, self.items)

    def __sub__(self, n):
        return self + -n

    @property
    def e(self):
        return self.pair * 2 + self.q

    @property
    def parity(self):
        return self.q % 2

    @property
    def turn(self):
        return self.pair + self.q // 2

    @property
    def exists(self):
        return not isinstance(self.pair, int) or 0 <= self.e < self.items


class NetworkBuffers:

    def __init__(self, nc, ctx, most_blocks):
        def sb(name, shape, dt=F32):
            return ctx.enter_context(nc.sbuf_tensor(name, shape, dt))

        nb = most_blocks
        self.ps = ctx.enter_context(nc.psum_tensor("ps_c", [P, 8, 512], F32))
        self.raw_gu = sb("raw_gu", [P, 2, 2, DC * F])
        self.raw_d = sb("raw_d", [P, 2, NF, D])
        self.gu_hi, self.gu_lo = (sb(n, [P, 2, 2, DC, F], F32R) for n in ("gu_hi", "gu_lo"))
        self.d_hi, self.d_lo = (sb(n, [P, 2, NF, D], F32R) for n in ("d_hi", "d_lo"))
        self.xg = sb("xg", [P, 2, nb, D])
        self.xt_hi, self.xt_lo = (sb(n, [P, 2, DC, nb * P], F32R) for n in ("xt_hi", "xt_lo"))
        self.sg, self.h = sb("sg", [P, 2, nb * P]), sb("h", [P, 2, nb * P])
        self.h_hi, self.h_lo = (sb(n, [P, 2, NF, nb * P], F32R) for n in ("h_hi", "h_lo"))
        self.y = sb("y", [P, 2, nb, D])
        self.ids_g, self.ids_s = sb("ids_g", [P, 2, nb], I32), sb("ids_s", [P, 2, nb], I32)
        self.wsl = sb("wsl", [P, 2, nb])
        self.ident = sb("ident_c", [P, P])
        self.slots = sb("slots", [P, E * CB, 2])
        self.ids = sb("ids", [P, E * CB], I32)
        self.w = sb("w", [P, E * CB])
        self.sh_ids = sb("sh_ids", [P, SHARED * (N // (2 * P)) * 2], I32)
        self.sh_w = sb("sh_w", [P, SHARED * (N // (2 * P)) * 2])


def network_section(nc, ctx, B, name, items, nb, wide, ids, weights, w_gu, w_d, weight_of, hbuf, out):
    W = nb * P
    ps = B.ps
    sets = 3 if nb == 2 else 2
    XT0, GU0, Y0 = 0, 2, 6
    if nb == 2:
        Y0 = 5

    def sem(what):
        return ctx.enter_context(nc.semaphore(f"{name}_{what}"))

    def sig(what, per):
        return Signal(sem(what), per)

    def pair_of(what, per):
        return [Signal(sem(f"{what}{p}"), per) for p in range(2)]

    gu_in, d_in = pair_of("gu_in", 16), pair_of("d_in", 32)
    rows_in = pair_of("rows_in", 16 * nb)
    added = sig("added", 16 * nb)
    gu_hi, gu_lo = sig("gu_hi", 2), sig("gu_lo", 2)
    d_hi, d_lo = sig("d_hi", 1), sig("d_lo", 1)
    xt_ready = sig("xt_ready", DC)
    xt_hi, xt_lo = sig("xt_hi", DC), sig("xt_lo", DC)
    gu_ready = sig("gu_ready", NF)
    sg_ready = sig("sg_ready", NF)
    h_ready = sig("h_ready", NF)
    h_hi, h_lo = sig("h_hi", NF), sig("h_lo", NF)
    w_ready = sig("w_ready", 1)
    y_ready = sig("y_ready", nb)
    y_taken = sig("y_taken", nb)
    passed = sem("passed")

    def drive(eng, before, slot, after):
        before(Item(0, 0, items))
        for q in range(2):
            slot(Item(0, q, items))
        with eng.Fori(1, items // 2 - 1) as pair:
            for q in range(2):
                slot(Item(pair, q, items))
        for q in range(2):
            slot(Item(items // 2 - 1, q, items))
        after(Item(items // 2 - 1, 1, items))

    none = lambda item: None

    def gu_banks(c, m):
        if nb == 2:
            bank = ps[0:m, GU0 + c % sets]
            return bank[:, 0:W], bank[:, W:2 * W]
        bank = GU0 + 2 * (c % sets)
        return ps[0:m, bank, 0:W], ps[0:m, bank + 1, 0:W]

    def chunk(item, c, back):
        n = c - back
        return item + n // NF, n % NF

    def sync_program(sp):
        def load(it):
            p = it.parity
            if (it - 2).exists:
                sp.wait_ge(gu_lo.sem, gu_lo.value((it - 2).e, 2))
            sp.dma_start(B.raw_gu[:, p].rearrange("p a n -> p (a n)"), w_gu(weight_of(it))).then_inc(gu_in[p].sem, 16)
            if (it - 2).exists:
                sp.wait_ge(d_lo.sem, d_lo.value((it - 2).e, 1))
            src = w_d(weight_of(it))
            sp.dma_start(B.raw_d[:, p, 0:2, :], src[0:2 * P, :].rearrange("(c p) n -> p c n", p=P)).then_inc(d_in[p].sem, 16)
            sp.dma_start(B.raw_d[0:FCH[2][1], p, 2, :], src[2 * P:F, :]).then_inc(d_in[p].sem, 16)
        drive(sp, none, load, none)

    def gather(pool, it):
        if not it.exists:
            return
        p = it.parity
        if (it - 2).exists:
            pool.wait_ge(rows_in[p].sem, rows_in[p].value((it - 2).turn, 16 * nb))
        pool.tensor_copy(B.ids_g[:, p, 0:nb], ids[:, bass.ds(it.e * wide, nb)])
        if (it - 2).exists:
            pool.wait_ge(xt_ready.sem, xt_ready.value((it - 2).e, DC))
            pool.sem_inc(passed, 1)
        pool.drain()
        for k in range(nb):
            pool.indirect_dma_start(
                out=B.xg[:, p, k, :], out_offset=None, in_=hbuf,
                in_offset=bass.IndirectOffsetOnAxis(B.ids_g[:, p, k:k + 1], 0),
                bounds_check=N - 1, oob_is_err=False).then_inc(rows_in[p].sem, 16)

    def pool_program(pool):
        def before(it):
            gather(pool, it)
            gather(pool, it + 1)

        def slot(it):
            p = it.parity
            gather(pool, it + 2)
            if (it - 1).exists:
                pool.wait_ge(added.sem, added.value((it - 1).e, 16 * nb))
            pool.tensor_copy(B.ids_s[:, p, 0:nb], ids[:, bass.ds(it.e * wide, nb)])
            pool.wait_ge(y_taken.sem, y_taken.value(it.e, nb))
            pool.sem_inc(passed, 1)
            pool.drain()
            for k in range(nb):
                pool.indirect_dma_start(
                    out=out, out_offset=bass.IndirectOffsetOnAxis(B.ids_s[:, p, k:k + 1], 0),
                    in_=B.y[:, p, k, :], in_offset=None, bounds_check=N - 1, oob_is_err=False,
                    compute_op=ALU.add).then_inc(added.sem, 16)

        drive(pool, before, slot, lambda it: pool.wait_ge(added.sem, added.value(it.e, 16 * nb)))

    HALVES = [(0, 0), (1, 1)]

    def cut_gu(eng, it, half, act):
        if not it.exists:
            return
        p = it.parity
        hi, raw = B.gu_hi[:, p, half], B.raw_gu[:, p, half].rearrange("p (c f) -> p c f", c=DC)
        if act:
            eng.wait_ge(gu_in[p].sem, gu_in[p].value(it.turn, 16))
            if (it - 2).exists:
                eng.wait_ge(gu_ready.sem, gu_ready.value((it - 2).e, NF))
            eng.activation(hi, raw, ACT.Copy).then_inc(gu_hi.sem, 1)
        else:
            eng.wait_ge(gu_hi.sem, gu_hi.value(it.e, half + 1))
            eng.tensor_tensor(B.gu_lo[:, p, half], raw, hi.bitcast(F32), ALU.subtract).then_inc(gu_lo.sem, 1)

    def cut_d(eng, it, act):
        p = it.parity
        if act:
            eng.wait_ge(d_in[p].sem, d_in[p].value(it.turn, 32))
            if (it - 2).exists:
                eng.wait_ge(y_ready.sem, y_ready.value((it - 2).e, nb))
            eng.activation(B.d_hi[:, p, 0:2], B.raw_d[:, p, 0:2], ACT.Copy)
            eng.activation(B.d_hi[0:96, p, 2], B.raw_d[0:96, p, 2], ACT.Copy).then_inc(d_hi.sem, 1)
        else:
            eng.wait_ge(d_hi.sem, d_hi.value(it.e, 1))
            eng.tensor_tensor(B.d_lo[:, p, 0:2], B.raw_d[:, p, 0:2], B.d_hi[:, p, 0:2].bitcast(F32), ALU.subtract)
            eng.tensor_tensor(B.d_lo[0:96, p, 2], B.raw_d[0:96, p, 2], B.d_hi[0:96, p, 2].bitcast(F32), ALU.subtract).then_inc(d_lo.sem, 1)

    def cut_x(eng, it, c, act):
        if not it.exists:
            return
        p = it.parity
        src = ps[:, XT0 + c % 2, 0:W]
        if act:
            eng.wait_ge(xt_ready.sem, xt_ready.value(it.e, c + 1))
            if c == 0 and (it - 2).exists:
                eng.wait_ge(gu_ready.sem, gu_ready.value((it - 2).e, NF))
            eng.activation(B.xt_hi[:, p, c, 0:W], src, ACT.Copy).then_inc(xt_hi.sem, 1)
        else:
            eng.wait_ge(xt_hi.sem, xt_hi.value(it.e, c + 1))
            eng.tensor_tensor(B.xt_lo[:, p, c, 0:W], src, B.xt_hi[:, p, c, 0:W].bitcast(F32), ALU.subtract).then_inc(xt_lo.sem, 1)

    def scalar_program(act):
        def before(it):
            cut_gu(act, it, 0, True)
            cut_gu(act, it, 1, True)
            for c in range(DC):
                cut_x(act, it, c, True)

        def silu(it, c):
            m = FCH[c][1]
            act.wait_ge(gu_ready.sem, gu_ready.value(it.e, c + 1))
            j, n = chunk(it, c, 2)
            if j.exists:
                act.wait_ge(h_ready.sem, h_ready.value(j.e, n + 1))
            act.activation(B.sg[0:m, (it.parity * NF + c) % 2, 0:W], gu_banks(c, m)[0], ACT.Silu).then_inc(sg_ready.sem, 1)

        def high(it, c):
            m = FCH[c][1]
            act.wait_ge(h_ready.sem, h_ready.value(it.e, c + 1))
            if c == 0 and (it - 2).exists:
                act.wait_ge(y_ready.sem, y_ready.value((it - 2).e, nb))
            act.activation(B.h_hi[0:m, it.parity, c, 0:W], B.h[0:m, (it.parity * NF + c) % 2, 0:W], ACT.Copy).then_inc(h_hi.sem, 1)

        def slot(it):
            cut_gu(act, it + 1, 0, True)
            silu(it, 0)
            cut_x(act, it + 1, 0, True)
            cut_x(act, it + 1, 1, True)
            high(it, 0)
            cut_gu(act, it + 1, 1, True)
            silu(it, 1)
            cut_x(act, it + 1, 2, True)
            cut_x(act, it + 1, 3, True)
            high(it, 1)
            cut_d(act, it, True)
            silu(it, 2)
            high(it, 2)
            results(it - 1)

        def results(it):
            if not it.exists:
                return
            act.wait_ge(w_ready.sem, w_ready.value(it.e, 1))
            if (it - 2).exists:
                act.wait_ge(added.sem, added.value((it - 2).e, 16 * nb))
            for k in range(nb):
                act.wait_ge(y_ready.sem, y_ready.value(it.e, k + 1))
                act.activation(B.y[:, it.parity, k, :], ps[:, Y0 + k % 2, :], ACT.Copy,
                                          scale=B.wsl[:, it.parity, k:k + 1]).then_inc(y_taken.sem, 1)

        drive(act, before, slot, results)

    def vector_program(dve):
        def before(it):
            cut_gu(dve, it, 0, False)
            cut_gu(dve, it, 1, False)
            for c in range(DC):
                cut_x(dve, it, c, False)

        def mix(it, c):
            m = FCH[c][1]
            dve.wait_ge(sg_ready.sem, sg_ready.value(it.e, c + 1))
            j, n = chunk(it, c, 2)
            if j.exists:
                dve.wait_ge(h_hi.sem, h_hi.value(j.e, n + 1))
            b = (it.parity * NF + c) % 2
            dve.tensor_tensor(B.h[0:m, b, 0:W], B.sg[0:m, b, 0:W], gu_banks(c, m)[1], ALU.mult).then_inc(h_ready.sem, 1)

        def rest(it, c):
            m = FCH[c][1]
            dve.wait_ge(h_hi.sem, h_hi.value(it.e, c + 1))
            dve.tensor_tensor(B.h_lo[0:m, it.parity, c, 0:W], B.h[0:m, (it.parity * NF + c) % 2, 0:W],
                                      B.h_hi[0:m, it.parity, c, 0:W].bitcast(F32), ALU.subtract).then_inc(h_lo.sem, 1)

        def slot(it):
            if (it - 2).exists:
                dve.wait_ge(y_taken.sem, y_taken.value((it - 2).e, nb))
            dve.tensor_copy(B.wsl[:, it.parity, 0:nb], weights[:, bass.ds(it.e * wide, nb)]).then_inc(w_ready.sem, 1)
            cut_gu(dve, it + 1, 0, False)
            mix(it, 0)
            cut_x(dve, it + 1, 0, False)
            cut_x(dve, it + 1, 1, False)
            rest(it, 0)
            cut_gu(dve, it + 1, 1, False)
            mix(it, 1)
            cut_x(dve, it + 1, 2, False)
            cut_x(dve, it + 1, 3, False)
            rest(it, 1)
            cut_d(dve, it, False)
            mix(it, 2)
            rest(it, 2)

        drive(dve, before, slot, none)

    def tensor_program(pe):
        def transpose_chunk(it, c):
            if not it.exists:
                return
            if c == 0:
                pe.wait_ge(rows_in[it.parity].sem, rows_in[it.parity].value(it.turn, 16 * nb))
            j, n = (it, c - 2) if c >= 2 else (it - 1, c + 2)
            if j.exists:
                pe.wait_ge(xt_lo.sem, xt_lo.value(j.e, n + 1))
            for k in range(nb):
                last = pe.transpose(ps[:, XT0 + c % 2, k * P:(k + 1) * P],
                                    B.xg[:, it.parity, k, c * P:(c + 1) * P], B.ident[:])
            last.then_inc(xt_ready.sem, 1)

        def gate_up(it, c):
            o, m = FCH[c]
            p = it.parity
            if c == 0:
                pe.wait_ge(gu_lo.sem, gu_lo.value(it.e, 2))
                pe.wait_ge(xt_lo.sem, xt_lo.value(it.e, DC))
            j, n = chunk(it, c, sets)
            if nb == 3 and c < 2:
                j, n = it - 1, (2 if c == 0 else 1)
            if j.exists:
                pe.wait_ge(h_ready.sem, h_ready.value(j.e, n + 1))
            for half in range(2):
                steps = [(w, x, d) for w, x in ((B.gu_hi, B.xt_hi), (B.gu_hi, B.xt_lo), (B.gu_lo, B.xt_hi))
                         for d in range(DC)]
                for i, (w, x, d) in enumerate(steps):
                    last = pe.matmul(gu_banks(c, m)[half], w[:, p, half, d, o:o + m], x[:, p, d, 0:W],
                                     start=i == 0, stop=i == len(steps) - 1)
            last.then_inc(gu_ready.sem, 1)

        def down(it):
            if not it.exists:
                return
            p = it.parity
            pe.wait_ge(d_lo.sem, d_lo.value(it.e, 1))
            pe.wait_ge(h_lo.sem, h_lo.value(it.e, NF))
            for k in range(nb):
                j, n = (it, k - 2) if k >= 2 else (it - 1, nb - 2 + k if nb == 2 else (2 if k == 0 else 1))
                if j.exists:
                    pe.wait_ge(y_taken.sem, y_taken.value(j.e, n + 1))
                steps = [(h, w, c) for h, w in ((B.h_hi, B.d_hi), (B.h_hi, B.d_lo), (B.h_lo, B.d_hi))
                         for c in range(NF)]
                for i, (h, w, c) in enumerate(steps):
                    m = FCH[c][1]
                    last = pe.matmul(ps[:, Y0 + k % 2, :], h[0:m, p, c, k * P:(k + 1) * P], w[0:m, p, c, :],
                                     start=i == 0, stop=i == len(steps) - 1)
                last.then_inc(y_ready.sem, 1)

        def before(it):
            for c in range(DC):
                transpose_chunk(it, c)

        def slot(it):
            gate_up(it, 0)
            transpose_chunk(it + 1, 0)
            transpose_chunk(it + 1, 1)
            gate_up(it, 1)
            transpose_chunk(it + 1, 2)
            transpose_chunk(it + 1, 3)
            gate_up(it, 2)
            down(it - 1)

        drive(pe, before, slot, down)

    return dict(sync=sync_program, gpsimd=pool_program, scalar=scalar_program,
                vector=vector_program, tensor=tensor_program)


def network_phase(nc, ins, out, hbuf, table, most):
    outer = ExitStack()
    with outer as ctx:
        B = NetworkBuffers(nc, ctx, CB)
        outf = out.rearrange("b s n -> (b s) n")
        tab_loaded, made = (ctx.enter_context(nc.semaphore(n)) for n in ("tab_loaded", "made"))
        blocks = N // (2 * P)
        with nc.Block() as block:
            @block.sync
            def _(sp):
                sp.dma_start(B.slots[:].rearrange("p n c -> p (n c)"),
                             table.rearrange("(p n) c -> p (n c)", p=P)).then_inc(tab_loaded, 16)

            @block.gpsimd
            def _(pool):
                pool.memset(B.ident[:], 0.0)
                pool.memset(B.xg[:], 0.0)
                pool.memset(B.sh_w[:], 1.0)
                pool.iota(B.sh_ids[:], [[0, SHARED], [P, 2 * blocks]], base=0, channel_multiplier=1)
                pool.drain()
                pool.affine_select(out=B.ident[:], in_=B.ident[:], compare_op=ALU.not_equal, fill=1.0,
                                   base=0, pattern=[[-1, P]], channel_multiplier=1)

            @block.vector
            def _(dve):
                dve.wait_ge(tab_loaded, 16)
                dve.tensor_copy(B.ids[:], B.slots[:, :, 0])
                dve.tensor_copy(B.w[:], B.slots[:, :, 1])

        shared = network_section(
            nc, ctx, B, "shared", SHARED * blocks, 2, 2, B.sh_ids, B.sh_w,
            lambda e: ins["sh_gu"][bass.ds(e, 1)].rearrange("a p n -> p (a n)"),
            lambda e: ins["sh_d"][bass.ds(e, 1)].rearrange("a f n -> (a f) n"),
            lambda it: it.e // blocks, hbuf, outf)
        expert = {
            nb: network_section(
                nc, ctx, B, f"expert{nb}", E, nb, CB, B.ids, B.w,
                lambda e: ins["w_gu"][bass.ds(e, 1)].rearrange("a p n -> p (a n)"),
                lambda e: ins["w_d"][bass.ds(e, 1)].rearrange("a f n -> (a f) n"),
                lambda it: it.e, hbuf, outf)
            for nb in (2, 3)}

        with nc.Block() as block:
            @block.sync
            def _(sp):
                shared["sync"](sp)

            @block.gpsimd
            def _(pool):
                shared["gpsimd"](pool)

            @block.scalar
            def _(act):
                shared["scalar"](act)

            @block.vector
            def _(dve):
                shared["vector"](dve)

            @block.tensor
            def _(pe):
                shared["tensor"](pe)

        def either(eng, what):
            rows = eng.value_load(most[0:1, 0:1], min_val=0, max_val=N)
            with eng.If(rows < 2 * P + 1):
                expert[2][what](eng)
            with eng.Else():
                expert[3][what](eng)

        with nc.Block() as block:
            @block.sync
            def _(sp):
                either(sp, "sync")

            @block.gpsimd
            def _(pool):
                either(pool, "gpsimd")

            @block.scalar
            def _(act):
                either(act, "scalar")

            @block.vector
            def _(dve):
                either(dve, "vector")

            @block.tensor
            def _(pe):
                either(pe, "tensor")


def program(nc, ins, out):
    with ExitStack() as ctx:
        most = ctx.enter_context(nc.sbuf_tensor("most", [P, 1], I32))
        hbuf = nc.dram_tensor("h2_rows", [N, D], F32, kind="Internal").ap()
        table = nc.dram_tensor("slot_table", [E * CAP, 2], F32, kind="Internal").ap()
        kvd = nc.dram_tensor("kv_dca", [NB * DCA, 2 * D], F32, kind="Internal").ap()
        attention_phase(nc, ins, out, hbuf, table, kvd, most)
        network_phase(nc, ins, out, hbuf, table, most)


def kernel(x, ctx_1024, L0_xattn_Wq, L0_xattn_bq, L0_xattn_Wk, L0_xattn_bk, L0_xattn_Wv, L0_xattn_bv,
           L0_xattn_Wkv_dca, L0_xattn_bkv_dca, L0_xattn_qn_w, L0_xattn_qn_b, L0_xattn_kn_w, L0_xattn_kn_b,
           L0_xattn_kn_dca_w, L0_xattn_kn_dca_b, L0_xattn_Wo, L0_xattn_bo, L0_ffn_gate_w, L0_ffn_w_gate,
           L0_ffn_w_up, L0_ffn_w_down, L0_ffn_sh_gate, L0_ffn_sh_up, L0_ffn_sh_down):
    import numpy as np
    from concourse import bacc
    from concourse.bass_utils import run_bass_kernel_spmd

    c = np.ascontiguousarray
    kv = np.concatenate([L0_xattn_Wk, L0_xattn_Wv], 1).reshape(DY, H, 2, HD)
    kvb = np.concatenate([L0_xattn_bk, L0_xattn_bv]).reshape(H, 2, HD)
    ctx_t = np.asarray(ctx_1024).transpose(0, 2, 1)

    def gate_up(gate, up):
        w = np.stack([gate, up], 1).reshape(-1, 2, F, DC, P)
        return c(w.transpose(0, 4, 1, 3, 2).reshape(-1, P, 2 * DC * F))

    arrays = dict(
        x=c(x), ctxT=c(ctx_t), ctx_dcaT=c(ctx_t[:, :, MAIN:].transpose(1, 0, 2).reshape(DY, NB * DCA)),
        Wq=c(L0_xattn_Wq), bq=c(L0_xattn_bq), Wk=c(kv[:, :, 0].reshape(DY, D)), bk=c(kvb[:, 0].reshape(D)),
        Wv=c(kv[:, :, 1].reshape(DY, D)), bv=c(kvb[:, 1].reshape(D)), Wkv_dca=c(L0_xattn_Wkv_dca),
        bkv_dca=c(L0_xattn_bkv_dca), qn_w=c(L0_xattn_qn_w), qn_b=c(L0_xattn_qn_b), kn_w=c(L0_xattn_kn_w),
        kn_b=c(L0_xattn_kn_b), kn_dca_w=c(L0_xattn_kn_dca_w), kn_dca_b=c(L0_xattn_kn_dca_b),
        Wo=c(L0_xattn_Wo), bo=c(L0_xattn_bo), gate_wT=c(np.asarray(L0_ffn_gate_w).T),
        w_gu=gate_up(np.asarray(L0_ffn_w_gate), np.asarray(L0_ffn_w_up)),
        w_d=c(np.asarray(L0_ffn_w_down).transpose(0, 2, 1)),
        sh_gu=gate_up(np.asarray(L0_ffn_sh_gate).reshape(SHARED, F, D), np.asarray(L0_ffn_sh_up).reshape(SHARED, F, D)),
        sh_d=c(np.asarray(L0_ffn_sh_down).T.reshape(SHARED, F, D)))
    nc = bacc.Bacc("TRN2", target_bir_lowering=False, num_devices=1)
    ins = {k: nc.dram_tensor(f"in_{k}", a.shape, mybir.dt.from_np(a.dtype), kind="ExternalInput").ap()
           for k, a in arrays.items()}
    out = nc.dram_tensor("out_0", (NB, S, D), F32, kind="ExternalOutput").ap()
    program(nc, ins, out)
    r = run_bass_kernel_spmd(nc, [{f"in_{k}": a for k, a in arrays.items()}], core_ids=[0])
    return r.results[0]["out_0"]
```

```python
from contextlib import ExitStack

import concourse.bass as bass
from concourse import mybir

ALU = mybir.AluOpType
ACT = mybir.ActivationFunctionType
F32 = mybir.dt.float32
F32R = mybir.dt.float32r
I32 = mybir.dt.int32
AX = mybir.AxisListType.X

P = 128
NB, S, D = 4, 512, 512
DY = 256
H, HD = 16, 32
DCA = 16
MAIN = S - DCA
T = S // P
DC, YC = D // P, DY // P
E, F, FS, TOPK = 64, 352, 704, 6
N = NB * S
CAP = 2 * ((N * TOPK + E - 1) // E)
CB = CAP // P
NF = 3
FCH = [(0, 128), (128, 128), (256, 96)]
SHARED = FS // F
NO_ROW = float(1 << 20)
SC = HD ** -0.5


class Signal:

    def __init__(self, sem, per, first=0):
        self.sem, self.per, self.first = sem, per, first

    def value(self, turn, n):
        return turn * self.per + (n + self.first)


def bc(ap, shape):
    return ap.broadcast_to(shape)


def attention_phase(nc, ins, out, hbuf, table, kvd, over):
    with ExitStack() as ctx:
        def sb(name, shape, dt=F32):
            return ctx.enter_context(nc.sbuf_tensor(name, shape, dt))

        def sem(name):
            return ctx.enter_context(nc.semaphore(name))

        def sig(name, per, first=0):
            return Signal(sem(name), per, first)

        ps = ctx.enter_context(nc.psum_tensor("ps_a", [P, 8, 512], F32))

        x = sb("x", [P, T, D])
        xh = sb("xh", [P, T, D])
        kt = sb("kt", [P, T, D])
        xT_hi, xT_lo = sb("xT_hi", [P, DC, S], F32R), sb("xT_lo", [P, DC, S], F32R)
        part3 = sb("part3", [P, 2, H, 3 * HD], F32R)
        qs = sb("qs", [P, H, S], F32R)
        ks = sb("ks", [P, H, S], F32R)
        v_main = sb("v_main", [P, T - 1, H, HD + 1])
        v_last = sb("v_last", [P, H, 2, HD + 1])
        prob = sb("prob", [P, 2, T, S])
        nmax = sb("nmax", [P, 2, T, 32], F32R)
        wq_hi, wq_lo = sb("wq_hi", [P, DC, D], F32R), sb("wq_lo", [P, DC, D], F32R)
        wo_hi, wo_lo = sb("wo_hi", [P, DC, D], F32R), sb("wo_lo", [P, DC, D], F32R)
        wk_hi, wk_lo = sb("wk_hi", [P, YC, D], F32R), sb("wk_lo", [P, YC, D], F32R)
        wv_hi, wv_lo = sb("wv_hi", [P, YC, D], F32R), sb("wv_lo", [P, YC, D], F32R)
        wg = sb("wg", [P, DC, E])
        bq, bk, bv, bo = (sb(n, [P, D]) for n in ("bq", "bk", "bv", "bo"))
        lnw = sb("lnw", [P, 6, HD])
        ident = sb("ident", [P, P])
        upper = sb("upper", [P, P])
        ones = sb("ones", [P, P])
        mv = sb("mv", [P, T, 2])
        bst = sb("bst", [P, T, 6])
        std = sb("std", [P, 4])
        rstd = sb("rstd", [P, 4])
        ss = sb("ss", [P, 2, T, H])
        rz = sb("rz", [P, T, 2])
        pv2 = sb("pv2", [P, 2, T, 2, HD])
        eps5, eps6 = sb("eps5", [P, 1]), sb("eps6", [P, 1])
        top = sb("top", [P, T, 8])
        carry = sb("carry", [P, T + 1, E])
        e3 = sb("e3", [P, E])
        code8 = sb("code8", [P, T, 8])
        slot = sb("slot", [P, T, 8], I32)
        rows = sb("rows", [P, T, TOPK, 2])
        row_id = sb("row_id", [P, T])
        lm, zs = sb("lm", [P, T]), sb("zs", [P, T])

        cT = kt[:, 0:YC, :]
        cT_hi, cT_lo = (part3[:, :, :, :].rearrange("p a h d -> p (a h d)")[:, i * YC * S:(i + 1) * YC * S]
                        .rearrange("p (c n) -> p c n", c=YC) for i in range(2))
        sq = prob[:, 1, 0:2, :]
        router = prob[:, 1].rearrange("p t n -> p (t n)")
        at = 0
        boards = []
        for width in (E + 2, E + 2, E, E, E, E):
            boards.append(router[:, at:at + T * width].rearrange("p (t e) -> p t e", t=T))
            at += T * width
        sco, rep, mask, wn, code, tmp = boards
        junk = router[:, at:at + E]
        slot_f = router[:, at + E:at + E + T * 8].rearrange("p (t k) -> p t k", t=T)

        sums = ss[:].rearrange("p a t h -> p (a t h)")
        stage = prob[:, :, :, :].rearrange("p a t n -> p (a t n)")
        wd_hi = qs[:, 0:4, :].rearrange("p h n -> p (h n)").rearrange("p (c n) -> p c n", c=YC)
        wd_lo = qs[:, 4:8, :].rearrange("p h n -> p (h n)").rearrange("p (c n) -> p c n", c=YC)
        cd = kt[:, 0, 0:YC * NB * DCA].rearrange("p (c n) -> p c n", c=YC)
        bd = kt[:, 1:3, :].rearrange("p t n -> p (t n)")
        cd_hi = qs[:, 8, 0:YC * NB * DCA].rearrange("p (c n) -> p c n", c=YC)
        cd_lo = qs[:, 9, 0:YC * NB * DCA].rearrange("p (c n) -> p c n", c=YC)
        kvd_rows = xh[:, 0:2, :].rearrange("p t n -> p (t n)")

        w1_in, w2_in, small_in, kvd_out, tab_out = (
            sem(n) for n in ("w1_in", "w2_in", "small_in", "kvd_out", "tab_out"))
        consts_done, act_pre, dve_pre, pe_pre = (
            sem(n) for n in ("consts_done", "act_pre", "dve_pre", "pe_pre"))

        def rowvec(v):
            return v.rearrange("(a n) -> a n", a=1)

        ND = NB * DCA
        with nc.Block() as block:
            @block.sync
            def _(sp):
                sp.dma_start(stage[:, 0:DC * D].rearrange("p (c n) -> p c n", c=DC),
                             ins["Wq"].rearrange("(c p) n -> p c n", p=P)).then_inc(w1_in, 16)
                sp.dma_start(stage[:, DC * D:2 * DC * D].rearrange("p (c n) -> p c n", c=DC),
                             ins["Wo"].rearrange("(c p) n -> p c n", p=P)).then_inc(w1_in, 16)
                for dst, v in ((bq, "bq"), (bk, "bk"), (bv, "bv"), (bo, "bo")):
                    sp.dma_start(dst[:], bc(rowvec(ins[v]), [P, D])).then_inc(small_in, 16)
                sp.dma_start(bd, bc(rowvec(ins["bkv_dca"]), [P, 2 * D])).then_inc(small_in, 16)
                for i, v in enumerate(("qn_w", "qn_b", "kn_w", "kn_b", "kn_w", "kn_b")):
                    rows_of = P if i < 4 else P - DCA
                    sp.dma_start(lnw[0:rows_of, i, :], bc(rowvec(ins[v]), [rows_of, HD])).then_inc(small_in, 16)
                for i, v in ((4, "kn_dca_w"), (5, "kn_dca_b")):
                    sp.dma_start(lnw[P - DCA:P, i, :], bc(rowvec(ins[v]), [DCA, HD])).then_inc(small_in, 16)
                sp.dma_start(wg[:], ins["gate_wT"].rearrange("(c p) n -> p c n", p=P)).then_inc(small_in, 16)
                sp.dma_start(cd, ins["ctx_dcaT"].rearrange("(c p) n -> p c n", p=P)).then_inc(small_in, 16)
                sp.wait_ge(dve_pre, 1)
                sp.dma_start(stage[:, 0:YC * D].rearrange("p (c n) -> p c n", c=YC),
                             ins["Wk"].rearrange("(c p) n -> p c n", p=P)).then_inc(w2_in, 16)
                sp.dma_start(stage[:, YC * D:2 * YC * D].rearrange("p (c n) -> p c n", c=YC),
                             ins["Wv"].rearrange("(c p) n -> p c n", p=P)).then_inc(w2_in, 16)
                sp.dma_start(stage[:, 2 * YC * D:4 * YC * D].rearrange("p (c n) -> p c n", c=YC),
                             ins["Wkv_dca"].rearrange("(c p) n -> p c n", p=P)).then_inc(w2_in, 16)
                sp.wait_ge(consts_done, 2)
                sp.dma_start(table.rearrange("(p n) c -> p (n c)", p=P),
                             xh[:, 3, 0:2 * E * CB]).then_inc(tab_out, 16)
                sp.wait_ge(dve_pre, 3)
                sp.dma_start(kvd, kvd_rows[0:ND, :]).then_inc(kvd_out, 16)
                sp.wait_ge(kvd_out, 16)
                sp.wait_ge(tab_out, 16)

            @block.gpsimd
            def _(pool):
                pool.memset(ident[:], 0.0)
                pool.memset(upper[:], 1.0)
                pool.memset(ones[:], 1.0)
                pool.memset(kt[:, 3, :], 0.0)
                pool.memset(xh[:, 3, :], 0.0)
                pool.memset(v_main[:], 1.0)
                pool.memset(v_last[:], 0.0)
                pool.memset(nmax[:].bitcast(F32), 0.0)
                pool.memset(eps5[:], 1e-5)
                pool.memset(eps6[:], 1e-6)
                pool.memset(carry[:], 0.0)
                pool.iota(row_id[:], [[P, T]], base=0, channel_multiplier=1,
                          allow_small_or_imprecise_dtypes=True)
                pool.iota(e3[:], [[CB, E]], base=1, channel_multiplier=0,
                          allow_small_or_imprecise_dtypes=True)
                pool.drain()
                pool.affine_select(out=ident[:], in_=ident[:], compare_op=ALU.not_equal, fill=1.0, base=0,
                                   pattern=[[-1, P]], channel_multiplier=1)
                pool.affine_select(out=upper[:], in_=upper[:], compare_op=ALU.is_gt, fill=0.0, base=0,
                                   pattern=[[1, P]], channel_multiplier=-1)
                pool.affine_select(out=kt[:, 3, 0:MAIN], in_=kt[:, 3, 0:MAIN], compare_op=ALU.not_equal,
                                   fill=1.0, base=-96, pattern=[[0, MAIN]], channel_multiplier=1)
                pool.affine_select(out=kt[:, 3, MAIN:S], in_=kt[:, 3, MAIN:S], compare_op=ALU.not_equal,
                                   fill=1.0, base=-97, pattern=[[0, DCA]], channel_multiplier=1)
                pool.affine_select(out=v_last[:, :, 0, HD:HD + 1], in_=v_last[:, :, 0, HD:HD + 1],
                                   compare_op=ALU.is_ge, fill=1.0, base=-(P - DCA), pattern=[[0, H]],
                                   channel_multiplier=1)
                pool.affine_select(out=v_last[:, :, 1, HD:HD + 1], in_=v_last[:, :, 1, HD:HD + 1],
                                   compare_op=ALU.is_gt, fill=1.0, base=P - DCA, pattern=[[0, H]],
                                   channel_multiplier=-1)
                empty = xh[:, 3, 0:2 * E * CB].rearrange("p (n c) -> p n c", c=2)
                pool.memset(empty[:, :, 0:1], NO_ROW)
                pool.drain().then_inc(consts_done, 2)

            def centre(dve, ap, groups):
                g = ap.rearrange("p (g d) -> p g d", d=HD)
                dve.tensor_reduce(sums[:, 0:groups], g, AX, ALU.add)
                dve.drain()
                dve.tensor_scalar(sums[:, 0:groups], sums[:, 0:groups], 1.0 / HD, None, ALU.mult)
                dve.drain()
                dve.tensor_tensor(g, g, bc(sums[:, 0:groups].unsqueeze(2), [P, groups, HD]), ALU.subtract)
                dve.drain()

            flat = lambda ap: ap.rearrange("p c n -> p (c n)")

            @block.vector
            def _(dve):
                def cut(hi, lo, src):
                    dve.tensor_copy(hi, src)
                    dve.drain()
                    dve.tensor_tensor(lo, src, hi.bitcast(F32), ALU.subtract)

                dve.wait_ge(w1_in, 32)
                centre(dve, stage[:, 0:DC * D], DC * H)
                cut(flat(wq_hi[:]), flat(wq_lo[:]), stage[:, 0:DC * D])
                cut(flat(wo_hi[:]), flat(wo_lo[:]), stage[:, DC * D:2 * DC * D])
                dve.drain().then_inc(dve_pre, 1)
                dve.wait_ge(small_in, 16 * 15)
                centre(dve, bq[:], H)
                centre(dve, bk[:], H)
                centre(dve, bd[:, 0:D], H)
                dve.tensor_scalar(lnw[:, 0:2, :], lnw[:, 0:2, :], SC, None, ALU.mult)
                cut(cd_hi, cd_lo, cd)
                dve.wait_ge(w2_in, 48)
                centre(dve, stage[:, 0:YC * D], YC * H)
                for c in range(YC):
                    o = 2 * YC * D + 2 * D * c
                    centre(dve, stage[:, o:o + D], H)
                cut(flat(wk_hi[:]), flat(wk_lo[:]), stage[:, 0:YC * D])
                cut(flat(wv_hi[:]), flat(wv_lo[:]), stage[:, YC * D:2 * YC * D])
                cut(flat(wd_hi), flat(wd_lo), stage[:, 2 * YC * D:4 * YC * D])
                dve.drain().then_inc(dve_pre, 1)
                dve.wait_ge(pe_pre, 1)
                for c in range(2):
                    dve.tensor_tensor(kvd_rows[0:ND, c * D:(c + 1) * D], ps[0:ND, c, :],
                                      bd[0:ND, c * D:(c + 1) * D], ALU.add)
                dve.drain().then_inc(dve_pre, 1)

            @block.scalar
            def _(act):
                act.wait_ge(consts_done, 2)
                act.wait_ge(pe_pre, 1)
                for h in range(H):
                    act.activation(ks[96:128, h, :], kt[96:128, 3, :], ACT.Copy)
                act.drain().then_inc(act_pre, 1)

            @block.tensor
            def _(pe):
                pe.wait_ge(dve_pre, 2)
                for c in range(2):
                    passes = [(a, w, y) for a, w in ((cd_hi, wd_hi), (cd_hi, wd_lo), (cd_lo, wd_hi))
                              for y in range(YC)]
                    for i, (a, w, y) in enumerate(passes):
                        last = pe.matmul(ps[0:ND, c, :], a[:, y, :], w[:, y, c * D:(c + 1) * D],
                                         start=i == 0, stop=i == len(passes) - 1)
                last.then_inc(pe_pre, 1)

        x_in, ctx_in, kd_in, vd_in, x1_out, h2_out = (
            sig(n, 16) for n in ("x_in", "ctx_in", "kd_in", "vd_in", "x1_out", "h2_out"))
        mean_ready = sig("mean_ready", 2)
        std_ready = sig("std_ready", 2)
        xh_ready = sig("xh_ready", T)
        tr_ready = sig("tr_ready", 3 * DC)
        hi_ready = sig("hi_ready", 3 * DC, first=1)
        lo_ready = sig("lo_ready", 2 * DC)
        ctx_hi, ctx_lo = sig("ctx_hi", 1), sig("ctx_lo", 1, first=1)
        proj_ready = sig("proj_ready", 3 * T)
        qk_raw = sig("qk_raw", 2 * T)
        v_ready = sig("v_ready", T)
        sq_ready = sig("sq_ready", 2 * T)
        ss_ready = sig("ss_ready", 2 * T, first=1)
        hstd_ready = sig("hstd_ready", 2)
        qk_norm = sig("qk_norm", 2 * T)
        qk_done = sig("qk_done", 2 * T, first=1)
        hi3_ready = sig("hi3_ready", 2 * T, first=1)
        lo3_ready = sig("lo3_ready", 2 * T, first=1)
        st_ready = sig("st_ready", 2 * T * 4, first=1)
        st_act = sig("st_act", 2 * T * 2)
        st_dve = sig("st_dve", 2 * T * 2)
        score_ready = sig("score_ready", H)
        nmax_ready = sig("nmax_ready", H)
        nmT_ready = sig("nmT_ready", H)
        nmT_in = sig("nmT_in", H)
        sT_ready = sig("sT_ready", H * T)
        prob_ready = sig("prob_ready", H * T)
        pv_ready = sig("pv_ready", H, first=1)
        pv_taken = sig("pv_taken", H)
        head_done = sig("head_done", H)
        xb_ready = sig("xb_ready", 1)
        att_ready = sig("att_ready", T, first=1)
        x1_ready = sig("x1_ready", T)
        h2_ready = sig("h2_ready", T)
        logit_ready = sig("logit_ready", 1)
        lmax_ready = sig("lmax_ready", 1)
        exp_ready = sig("exp_ready", 1)
        mask_ready = sig("mask_ready", 1)
        pos_ready = sig("pos_ready", 1)
        tab_sent = sig("tab_sent", 1, first=1)
        slot_ready = sig("slot_ready", 1, first=1)
        tab_in = sig("tab_in", 16 * T * TOPK)

        given = dict(vector=(ctx_lo, lo3_ready, ss_ready, slot_ready), gpsimd=(qk_done, tab_sent),
                     tensor=(pv_ready, st_ready, att_ready), scalar=(hi3_ready, hi_ready))
        dve_passed, sp_passed = sem("dve_passed"), sem("sp_passed")
        passed = sem("passed")

        def give_first(eng, name):
            for s in given[name]:
                eng.sem_inc(s.sem, 1)


        HI_LO = lambda a_hi, a_lo, b_hi, b_lo: ((a_hi, b_hi), (a_hi, b_lo), (a_lo, b_hi))
        PROJ, TRB, STB, POB = 4, 6, 4, 7

        with nc.Block() as block:
            @block.sync
            def _(sp):
                with sp.Fori(0, NB) as b:
                    sp.dma_start(x[:], ins["x"][bass.ds(b, 1)].rearrange("a (t p) n -> p (a t) n", p=P)).then_inc(x_in.sem, 16)
                    sp.wait_ge(ctx_lo.sem, ctx_lo.value(b, 0))
                    sp.dma_start(cT, ins["ctxT"][bass.ds(b, 1)].rearrange("a (c p) n -> p (a c) n", p=P)).then_inc(ctx_in.sem, 16)
                    sp.wait_ge(qk_done.sem, qk_done.value(b, 0))
                    sp.dma_start(kt[P - DCA:P, T - 1, :], kvd[bass.ds(b * DCA, DCA), 0:D]).then_inc(kd_in.sem, 16)
                    sp.wait_ge(pv_ready.sem, pv_ready.value(b, 0))
                    sp.dma_start(v_last[P - DCA:P, :, 1, 0:HD],
                                          kvd[bass.ds(b * DCA, DCA), D:2 * D].rearrange("p (h d) -> p h d", d=HD)).then_inc(vd_in.sem, 16)
                    sp.wait_ge(x1_ready.sem, x1_ready.value(b, T))
                    sp.dma_start(out[bass.ds(b, 1)].rearrange("a (t p) n -> p (a t) n", p=P), x[:]).then_inc(x1_out.sem, 16)
                    sp.wait_ge(h2_ready.sem, h2_ready.value(b, T))
                    sp.dma_start(hbuf[bass.ds(b * S, S), :].rearrange("(t p) n -> p t n", p=P), xh[:]).then_inc(h2_out.sem, 16)
                    sp.wait_ge(x1_out.sem, x1_out.value(b, 16))
                    sp.wait_ge(h2_out.sem, h2_out.value(b, 16))
                    sp.sem_inc(sp_passed, 1)

            @block.gpsimd
            def _(pool):
                give_first(pool, "gpsimd")
                with pool.Fori(0, NB) as b:
                    pool.wait_ge(xh_ready.sem, xh_ready.value(b, T))
                    pool.tensor_tensor(x[:], x[:], bc(bo[:].unsqueeze(1), [P, T, D]), ALU.add).then_inc(xb_ready.sem, 1)
                    for u in range(2 * T):
                        pool.wait_ge(qk_norm.sem, qk_norm.value(b, u + 1))
                        t, src = u % T, (xh if u < T else kt)
                        i = 0 if u < T else 2 if t < T - 1 else 4
                        v = src[:, t, :].rearrange("p (h d) -> p h d", d=HD)
                        pool.tensor_tensor(v, v, bc(lnw[:, i, :].unsqueeze(1), [P, H, HD]), ALU.mult)
                        pool.drain()
                        pool.tensor_tensor(v, v, bc(lnw[:, i + 1, :].unsqueeze(1), [P, H, HD]), ALU.add).then_inc(qk_done.sem, 1)
                    for h in range(H):
                        pool.wait_ge(pv_taken.sem, pv_taken.value(b, h + 1))
                        if h == 0:
                            pool.wait_ge(lo3_ready.sem, lo3_ready.value(b, T))
                            pool.wait_ge(hi3_ready.sem, hi3_ready.value(b, T))
                        pool.tensor_tensor(xh[:, :, h * HD:(h + 1) * HD], pv2[:, h % 2, :, 0, :],
                                                        pv2[:, h % 2, :, 1, :], ALU.add).then_inc(head_done.sem, 1)
                    pool.wait_ge(slot_ready.sem, slot_ready.value(b, 1))
                    pool.sem_inc(passed, 1)
                    for t in range(T):
                        for k in range(TOPK):
                            pool.indirect_dma_start(
                                out=table, out_offset=bass.IndirectOffsetOnAxis(slot[:, t, k:k + 1], 0),
                                in_=rows[:, t, k, :], in_offset=None, bounds_check=E * CAP - 1,
                                oob_is_err=False).then_inc(tab_in.sem, 16)
                    pool.wait_ge(tab_in.sem, tab_in.value(b, 16 * T * TOPK))
                    pool.sem_inc(tab_sent.sem, 1)

            def layer_stats(dve, b, ready, order):
                for t in range(T):
                    ready(t)
                    dve.bn_stats(bst[:, t, :], x[:, t, :])
                dve.drain()
                for t in range(T):
                    dve.bn_aggr(mv[:, t, :], bst[:, t, :])
                dve.drain().then_inc(mean_ready.sem, 1)
                dve.wait_ge(std_ready.sem, std_ready.value(b, order + 1))
                dve.reciprocal(rstd[:], std[:])
                dve.drain()

            @block.vector
            def _(dve):
                give_first(dve, "vector")
                with dve.Fori(0, NB) as b:
                    dve.wait_ge(x_in.sem, x_in.value(b, 16))
                    layer_stats(dve, b, lambda t: None, 0)
                    for t in range(T):
                        dve.tensor_scalar(xh[:, t, :], x[:, t, :], mv[:, t, 0:1], rstd[:, t:t + 1],
                                                      ALU.subtract, ALU.mult).then_inc(xh_ready.sem, 1)
                    dve.wait_ge(ctx_hi.sem, ctx_hi.value(b, 1))
                    dve.tensor_tensor(cT_lo[:, :, 0:MAIN], cT[:, :, 0:MAIN], cT_hi[:, :, 0:MAIN].bitcast(F32), ALU.subtract).then_inc(ctx_lo.sem, 1)
                    for c in range(DC):
                        dve.wait_ge(hi_ready.sem, hi_ready.value(b, c + 1))
                        dve.tensor_tensor(xT_lo[:, c, :], ps[:, c, :], xT_hi[:, c, :].bitcast(F32), ALU.subtract).then_inc(lo_ready.sem, 1)
                    for u in range(2 * T):
                        dve.wait_ge(proj_ready.sem, proj_ready.value(b, u + 1))
                        t = u % T
                        m = P - DCA if u == 2 * T - 1 else P
                        dst, bias = (xh, bq) if u < T else (kt, bk)
                        if u == 0:
                            dve.wait_ge(tr_ready.sem, tr_ready.value(b, DC))
                        if u == T:
                            dve.wait_ge(lo3_ready.sem, lo3_ready.value(b, 0))
                            dve.wait_ge(hi3_ready.sem, hi3_ready.value(b, 0))
                        dve.tensor_tensor(dst[0:m, t, :], ps[0:m, PROJ + u % 2, :], bias[0:m, :], ALU.add).then_inc(qk_raw.sem, 1)
                    for half, src in ((0, xh), (1, kt)):
                        for t in range(T):
                            dve.wait_ge(sq_ready.sem, sq_ready.value(b, half * T + t + 1))
                            dve.tensor_reduce(ss[:, half, t, :],
                                                          sq[:, t % 2, :].rearrange("p (h d) -> p h d", d=HD), AX, ALU.add).then_inc(ss_ready.sem, 1)
                        dve.wait_ge(hstd_ready.sem, hstd_ready.value(b, half + 1))
                        dve.reciprocal(ss[:, half], ss[:, half])
                        dve.drain()
                        for t in range(T):
                            v = src[:, t, :].rearrange("p (h d) -> p h d", d=HD)
                            dve.tensor_tensor(v, v, bc(ss[:, half, t, :].unsqueeze(2), [P, H, HD]), ALU.mult).then_inc(qk_norm.sem, 1)
                    for t in range(T):
                        dve.wait_ge(proj_ready.sem, proj_ready.value(b, 2 * T + t + 1))
                        m = P - DCA if t == T - 1 else P
                        dst = v_main[:, t, :, 0:HD] if t < T - 1 else v_last[0:m, :, 0, 0:HD]
                        dve.tensor_tensor(dst, ps[0:m, PROJ + t % 2, :].rearrange("p (h d) -> p h d", d=HD),
                                                     bv[0:m, :].rearrange("p (h d) -> p h d", d=HD), ALU.add).then_inc(v_ready.sem, 1)
                    for u in range(2 * T):
                        src, at = (xh, 2) if u < T else (kt, 1)
                        dve.wait_ge(hi3_ready.sem, hi3_ready.value(b, u + 1))
                        dve.tensor_tensor(part3[:, u % 2, :, at * HD:(at + 1) * HD],
                                                       src[:, u % T, :].rearrange("p (h d) -> p h d", d=HD),
                                                       part3[:, u % 2, :, 0:HD].bitcast(F32), ALU.subtract).then_inc(lo3_ready.sem, 1)
                        for g in (1, 3):
                            dve.wait_ge(st_ready.sem, st_ready.value(b, 4 * u + g + 1))
                            dst = (qs if u < T else ks)[0:96, 4 * g:4 * g + 4, (u % T) * P:(u % T + 1) * P]
                            dve.tensor_copy(dst, ps[0:96, g, :].rearrange("p (h n) -> p h n", n=P)).then_inc(st_dve.sem, 1)
                    def maxima(h):
                        dve.wait_ge(score_ready.sem, score_ready.value(b, h + 1))
                        if h >= 2:
                            dve.wait_ge(nmT_ready.sem, nmT_ready.value(b, h - 1))
                        dve.tensor_reduce(nmax[:, h % 2, :, 0], ps[:, 0:T, 0:MAIN], AX, ALU.max, negate=True)
                        dve.tensor_reduce(nmax[:, h % 2, :, 1], ps[:, 0:T, MAIN:S], AX, ALU.max, negate=True)
                        dve.drain().then_inc(nmax_ready.sem, 1)

                    maxima(0)
                    for h in range(H + 1):
                        if h + 1 < H:
                            maxima(h + 1)
                        if h >= 1:
                            g = h - 1
                            dve.wait_ge(pv_ready.sem, pv_ready.value(b, g + 1))
                            pv = ps[:, POB, 0:T * 2 * (HD + 1)].rearrange("p (t c d) -> p t c d", t=T, c=2)
                            if g >= 2:
                                dve.wait_ge(head_done.sem, head_done.value(b, g - 1))
                            dve.reciprocal(rz[:], pv[:, :, :, HD])
                            dve.drain()
                            dve.tensor_tensor(pv2[:, g % 2], pv[:, :, :, 0:HD],
                                                          bc(rz[:].unsqueeze(3), [P, T, 2, HD]), ALU.mult).then_inc(pv_taken.sem, 1)
                    for c in range(DC):
                        dve.wait_ge(hi_ready.sem, hi_ready.value(b, DC + c + 1))
                        dve.tensor_tensor(xT_lo[:, c, :], ps[:, c, :], xT_hi[:, c, :].bitcast(F32), ALU.subtract).then_inc(lo_ready.sem, 1)
                    dve.wait_ge(xb_ready.sem, xb_ready.value(b, 1))

                    def residual(t):
                        dve.wait_ge(att_ready.sem, att_ready.value(b, t + 1))
                        dve.tensor_tensor(x[:, t, :], ps[:, PROJ + t % 2, :], x[:, t, :], ALU.add).then_inc(x1_ready.sem, 1)
                        dve.drain()

                    layer_stats(dve, b, residual, 1)
                    for t in range(T):
                        dve.tensor_scalar(xh[:, t, :], x[:, t, :], mv[:, t, 0:1], rstd[:, t:t + 1],
                                                      ALU.subtract, ALU.mult).then_inc(h2_ready.sem, 1)
                    dve.wait_ge(logit_ready.sem, logit_ready.value(b, 1))
                    logits = ps[:, 5, 0:T * E].rearrange("p (t e) -> p t e", e=E)
                    dve.tensor_reduce(lm[:], logits, AX, ALU.max, negate=True)
                    dve.drain().then_inc(lmax_ready.sem, 1)
                    dve.wait_ge(exp_ready.sem, exp_ready.value(b, 1))
                    dve.memset(sco[:, :, E:E + 1], -1.0)
                    dve.memset(sco[:, :, E + 1:E + 2], -2.0)
                    dve.reciprocal(zs[:], zs[:])
                    dve.drain()
                    probs = sco[:, :, 0:E]
                    dve.tensor_tensor(probs, probs, bc(zs[:].unsqueeze(2), [P, T, E]), ALU.mult)
                    dve.drain()
                    for t in range(T):
                        dve.max(top[:, t, :], sco[:, t, 0:E])
                    dve.drain()
                    dve.tensor_reduce(lm[:], top[:, :, 0:TOPK], AX, ALU.add)
                    dve.memset(top[:, :, 6:7], -1.0)
                    dve.memset(top[:, :, 7:8], -2.0)
                    dve.drain()
                    dve.tensor_scalar(lm[:], lm[:], 1e-20, None, ALU.add)
                    for t in range(T):
                        dve.match_replace(rep[:, t, :], top[:, t, :], sco[:, t, :], -3.0)
                    dve.drain()
                    dve.reciprocal(lm[:], lm[:])
                    dve.tensor_scalar(mask, rep[:, :, 0:E], -2.5, None, ALU.is_lt)
                    dve.tensor_copy(carry[:, 0, :], carry[:, T, :])
                    dve.drain()
                    for t in range(T):
                        dve.tensor_tensor(carry[:, t + 1, :], carry[:, t, :], mask[:, t, :], ALU.add)
                        dve.drain()
                    dve.tensor_tensor(wn[:], probs, bc(lm[:].unsqueeze(2), [P, T, E]), ALU.mult).then_inc(mask_ready.sem, 1)
                    dve.wait_ge(pos_ready.sem, pos_ready.value(b, 1))
                    pos = ps[:, 5, 0:T * E].rearrange("p (t e) -> p t e", e=E)
                    dve.tensor_scalar(code, pos, float(E * CB), None, ALU.mult)
                    dve.tensor_scalar(tmp, pos, float(P) - 0.5, -float(P * E * CB - 1), ALU.is_gt, ALU.mult)
                    dve.drain()
                    dve.tensor_tensor(code, code, tmp, ALU.add)
                    dve.drain()
                    dve.tensor_scalar(tmp, pos, 2.0 * P - 0.5, -float(P * E * CB - 1), ALU.is_gt, ALU.mult)
                    dve.drain()
                    dve.tensor_tensor(code, code, tmp, ALU.add)
                    dve.drain()
                    dve.tensor_tensor(code, code, bc(e3[:].unsqueeze(1), [P, T, E]), ALU.add)
                    dve.tensor_scalar(tmp, pos, float(CAP) - 0.5, None, ALU.is_lt)
                    dve.drain()
                    dve.tensor_tensor(tmp, tmp, mask, ALU.mult)
                    dve.drain()
                    dve.wait_ge(tab_sent.sem, tab_sent.value(b, 0))
                    dve.tensor_tensor(code, code, tmp, ALU.mult)
                    dve.drain()
                    for t in range(T):
                        dve.max(code8[:, t, :], code[:, t, :])
                    dve.drain()
                    dve.tensor_scalar(slot_f, code8[:], 0.5, NO_ROW, ALU.is_lt, ALU.mult)
                    dve.tensor_copy(rows[:, :, :, 0], bc(row_id[:].unsqueeze(2), [P, T, TOPK]))
                    for t in range(T):
                        for k in range(TOPK):
                            dve.scalar_tensor_tensor(junk, code[:, t, :], code8[:, t, k:k + 1], wn[:, t, :],
                                                     ALU.is_equal, ALU.mult, accum_out=rows[:, t, k, 1:2])
                            dve.drain()
                    dve.tensor_tensor(slot_f, slot_f, code8[:], ALU.add)
                    dve.tensor_scalar(row_id[:], row_id[:], float(S), None, ALU.add)
                    dve.drain()
                    dve.tensor_scalar(slot[:], slot_f, -1.0, None, ALU.add)
                    dve.drain().then_inc(slot_ready.sem, 1)
                    dve.wait_ge(h2_out.sem, h2_out.value(b, 16))
                    dve.sem_inc(dve_passed, 1)

            def take(act, b, u):
                for g in (0, 2):
                    act.wait_ge(st_ready.sem, st_ready.value(b, 4 * u + g + 1))
                    dst = (qs if u < T else ks)[0:96, 4 * g:4 * g + 4, (u % T) * P:(u % T + 1) * P]
                    act.activation(dst, ps[0:96, g, :].rearrange("p (h n) -> p h n", n=P), ACT.Copy).then_inc(st_act.sem, 1)

            @block.scalar
            def _(act):
                give_first(act, "scalar")
                with act.Fori(0, NB) as b:
                    act.wait_ge(mean_ready.sem, mean_ready.value(b, 1))
                    act.activation(std[:], mv[:, :, 1], ACT.Sqrt, bias=eps5[:]).then_inc(std_ready.sem, 1)
                    act.wait_ge(ctx_in.sem, ctx_in.value(b, 16))
                    act.wait_ge(st_ready.sem, st_ready.value(b, 0))
                    act.activation(cT_hi[:, :, 0:MAIN], cT[:, :, 0:MAIN], ACT.Copy).then_inc(ctx_hi.sem, 1)
                    for c in range(DC):
                        act.wait_ge(tr_ready.sem, tr_ready.value(b, c + 1))
                        act.wait_ge(att_ready.sem, att_ready.value(b, 0))
                        act.activation(xT_hi[:, c, :], ps[:, c, :], ACT.Copy).then_inc(hi_ready.sem, 1)
                    act.wait_ge(kd_in.sem, kd_in.value(b, 16))
                    for half, src in ((0, xh), (1, kt)):
                        for t in range(T):
                            u = half * T + t
                            act.wait_ge(qk_raw.sem, qk_raw.value(b, u + 1))
                            if u >= 2:
                                act.wait_ge(ss_ready.sem, ss_ready.value(b, u - 1))
                            else:
                                act.wait_ge(ss_ready.sem, ss_ready.value(b, 0))
                            act.activation(sq[:, t % 2, :], src[:, t, :], ACT.Square).then_inc(sq_ready.sem, 1)
                        act.wait_ge(ss_ready.sem, ss_ready.value(b, (half + 1) * T))
                        act.activation(ss[:, half], ss[:, half], ACT.Sqrt, bias=eps6[:], scale=1.0 / HD).then_inc(hstd_ready.sem, 1)
                    for u in range(2 * T):
                        src = xh if u < T else kt
                        act.wait_ge(qk_done.sem, qk_done.value(b, u + 1))
                        if u == 0:
                            act.wait_ge(proj_ready.sem, proj_ready.value(b, 3 * T))
                        if u >= 2:
                            act.wait_ge(st_ready.sem, st_ready.value(b, 4 * (u - 1)))
                        v = src[:, u % T, :].rearrange("p (h d) -> p h d", d=HD)
                        other = 1 if u < T else 2
                        act.activation(part3[:, u % 2, :, 0:HD], v, ACT.Copy)
                        act.activation(part3[:, u % 2, :, other * HD:(other + 1) * HD], v, ACT.Copy).then_inc(hi3_ready.sem, 1)
                        if u >= 1:
                            take(act, b, u - 1)
                    take(act, b, 2 * T - 1)
                    for h in range(H):
                        act.wait_ge(nmT_ready.sem, nmT_ready.value(b, h + 1))
                        act.activation(qs[96:128, h, :], ps[0:32, TRB, :], ACT.Copy).then_inc(nmT_in.sem, 1)
                        for c in range(T):
                            act.wait_ge(sT_ready.sem, sT_ready.value(b, h * T + c + 1))
                            if h >= 2 and c == 0:
                                act.wait_ge(pv_ready.sem, pv_ready.value(b, h - 1))
                            act.activation(prob[:, h % 2, c, :], ps[:, STB + c % 2, :], ACT.Exp).then_inc(prob_ready.sem, 1)
                    for c in range(DC):
                        act.wait_ge(tr_ready.sem, tr_ready.value(b, DC + c + 1))
                        act.activation(xT_hi[:, c, :], ps[:, c, :], ACT.Copy).then_inc(hi_ready.sem, 1)
                    act.wait_ge(mean_ready.sem, mean_ready.value(b, 2))
                    act.activation(std[:], mv[:, :, 1], ACT.Sqrt, bias=eps5[:]).then_inc(std_ready.sem, 1)
                    for c in range(DC):
                        act.wait_ge(tr_ready.sem, tr_ready.value(b, 2 * DC + c + 1))
                        act.activation(prob[:, 0, c, :], ps[:, c, :], ACT.Copy).then_inc(hi_ready.sem, 1)
                    act.wait_ge(lmax_ready.sem, lmax_ready.value(b, 1))
                    for t in range(T):
                        act.activation(sco[:, t, 0:E], ps[:, 5, t * E:(t + 1) * E], ACT.Exp,
                                       bias=lm[:, t:t + 1], accum_out=zs[:, t:t + 1])
                    act.drain().then_inc(exp_ready.sem, 1)

            @block.tensor
            def _(pe):
                def transpose_rows(b, ready, of, base):
                    for c in range(DC):
                        for t in range(T):
                            if c == 0:
                                ready(t)
                            last = pe.transpose(ps[:, c, t * P:(t + 1) * P], of[:, t, c * P:(c + 1) * P], ident[:])
                        last.then_inc(tr_ready.sem, 1)

                def product(dst, m, t, pairs, chunks, done):
                    steps = [(l, r, c) for l, r in pairs for c in range(chunks)]
                    for i, (l, r, c) in enumerate(steps):
                        last = pe.matmul(dst, l[:, c, t * P:t * P + m], r[:, c, :],
                                         start=i == 0, stop=i == len(steps) - 1)
                    last.then_inc(done.sem, 1)

                give_first(pe, "tensor")
                with pe.Fori(0, NB) as b:
                    pe.wait_ge(hi_ready.sem, hi_ready.value(b, 0))
                    transpose_rows(b, lambda t: pe.wait_ge(xh_ready.sem, xh_ready.value(b, t + 1)), xh, 0)
                    pos_free = slot_ready
                    pe.wait_ge(pos_free.sem, pos_free.value(b, 0))
                    for u in range(3 * T):
                        t = u % T
                        m = P - DCA if u >= T and t == T - 1 else P
                        if u == 0:
                            pe.wait_ge(lo_ready.sem, lo_ready.value(b, DC))
                        if u == T:
                            pe.wait_ge(ctx_lo.sem, ctx_lo.value(b, 1))
                        if 2 <= u:
                            if u - 2 < 2 * T:
                                pe.wait_ge(qk_raw.sem, qk_raw.value(b, u - 1))
                            else:
                                pe.wait_ge(v_ready.sem, v_ready.value(b, u - 1 - 2 * T))
                        dst = ps[0:m, PROJ + u % 2, :]
                        if u < T:
                            product(dst, m, t, HI_LO(xT_hi, xT_lo, wq_hi, wq_lo), DC, proj_ready)
                        elif u < 2 * T:
                            product(dst, m, t, HI_LO(cT_hi, cT_lo, wk_hi, wk_lo), YC, proj_ready)
                        else:
                            product(dst, m, t, HI_LO(cT_hi, cT_lo, wv_hi, wv_lo), YC, proj_ready)
                    for u in range(2 * T):
                        pe.wait_ge(lo3_ready.sem, lo3_ready.value(b, u + 1))
                        for g in range(4):
                            if u == 0 and g == 0:
                                pe.wait_ge(lo_ready.sem, lo_ready.value(b, DC))
                            if u >= 1:
                                if g % 2:
                                    pe.wait_ge(st_dve.sem, st_dve.value(b, 2 * (u - 1) + g // 2 + 1))
                                else:
                                    pe.wait_ge(st_act.sem, st_act.value(b, 2 * (u - 1) + g // 2 + 1))
                            for i in range(4):
                                h = 4 * g + i
                                last = pe.transpose(ps[0:96, g, i * P:(i + 1) * P], part3[:, u % 2, h, :].bitcast(F32), ident[:])
                            last.then_inc(st_ready.sem, 1)
                    pe.wait_ge(st_act.sem, st_act.value(b, 4 * T))
                    pe.wait_ge(st_dve.sem, st_dve.value(b, 4 * T))
                    pe.wait_ge(v_ready.sem, v_ready.value(b, T))
                    pe.wait_ge(vd_in.sem, vd_in.value(b, 16))

                    def scores(h):
                        for t in range(T):
                            last = pe.matmul(ps[:, t, :], qs[0:96, h, t * P:(t + 1) * P], ks[0:96, h, :], start=True, stop=True)
                        last.then_inc(score_ready.sem, 1)

                    def weigh(h, t):
                        prow = prob[:, h % 2, :, t * P:(t + 1) * P]
                        o = t * 2 * (HD + 1)
                        pe.matmul(ps[:, POB, o:o + 2 * (HD + 1)], prow[:, T - 1, :],
                                  v_last[:, h].rearrange("p c d -> p (c d)"), start=True, stop=False)
                        for c in range(T - 1):
                            last = pe.matmul(ps[:, POB, o:o + HD + 1], prow[:, c, :], v_main[:, c, h, :],
                                             start=False, stop=c == T - 2)
                        return last

                    scores(0)
                    for h in range(H + 1):
                        if h < H:
                            pe.wait_ge(nmax_ready.sem, nmax_ready.value(b, h + 1))
                            if h >= 1:
                                pe.wait_ge(nmT_in.sem, nmT_in.value(b, h))
                            for t in range(T):
                                last = pe.transpose(ps[0:32, TRB, t * P:(t + 1) * P], nmax[:, h % 2, t, :].bitcast(F32), ident[:])
                            last.then_inc(nmT_ready.sem, 1)
                            if h + 1 < H:
                                scores(h + 1)
                            pe.wait_ge(nmT_in.sem, nmT_in.value(b, h + 1))
                        if h >= 1:
                            pe.wait_ge(prob_ready.sem, prob_ready.value(b, h * T))
                            if h >= 2:
                                pe.wait_ge(pv_taken.sem, pv_taken.value(b, h - 1))
                        for c in range(T):
                            if h < H:
                                if h * T + c >= 2:
                                    pe.wait_ge(prob_ready.sem, prob_ready.value(b, h * T + c - 1))
                                pe.matmul(ps[:, STB + c % 2, :], ks[:, h, c * P:(c + 1) * P], qs[:, h, :], start=True, stop=True).then_inc(sT_ready.sem, 1)
                            if h >= 1:
                                last = weigh(h - 1, c)
                        if h >= 1:
                            last.then_inc(pv_ready.sem, 1)
                    transpose_rows(b, lambda t: pe.wait_ge(head_done.sem, head_done.value(b, H)), xh, DC)
                    for t in range(T):
                        if t == 0:
                            pe.wait_ge(lo_ready.sem, lo_ready.value(b, 2 * DC))
                        if t >= 2:
                            pe.wait_ge(x1_ready.sem, x1_ready.value(b, t - 1))
                        product(ps[:, PROJ + t % 2, :], P, t, HI_LO(xT_hi, xT_lo, wo_hi, wo_lo), DC, att_ready)
                    transpose_rows(b, lambda t: pe.wait_ge(h2_ready.sem, h2_ready.value(b, t + 1)), xh, 2 * DC)
                    pe.wait_ge(hi_ready.sem, hi_ready.value(b, 3 * DC))
                    pe.wait_ge(x1_ready.sem, x1_ready.value(b, T))
                    for t in range(T):
                        for c in range(DC):
                            last = pe.matmul(ps[:, 5, t * E:(t + 1) * E], prob[:, 0, c, t * P:(t + 1) * P], wg[:, c, :],
                                             start=c == 0, stop=c == DC - 1)
                    last.then_inc(logit_ready.sem, 1)
                    pe.wait_ge(mask_ready.sem, mask_ready.value(b, 1))
                    for t in range(T):
                        pe.matmul(ps[:, 5, t * E:(t + 1) * E], upper[:], mask[:, t, :], start=True, stop=False)
                        last = pe.matmul(ps[:, 5, t * E:(t + 1) * E], ones[:], carry[:, t, :], start=False, stop=True)
                    last.then_inc(pos_ready.sem, 1)

        numbered, counted, marked, ranked, listed = (
            sem(n) for n in ("numbered", "counted", "marked", "ranked", "listed"))
        number, place = row_id, e3
        marks = mask[0:E, 0, :]
        is_over, rank = lm[0:E, 0:1], lm[0:E, 1:2]
        with nc.Block() as block:
            @block.gpsimd
            def _(pool):
                pool.iota(number[:, 0:1], [[P, 1]], base=0, channel_multiplier=1,
                          allow_small_or_imprecise_dtypes=True)
                pool.iota(place[:], [[1, E]], base=0, channel_multiplier=0,
                          allow_small_or_imprecise_dtypes=True).then_inc(numbered, 1)

            @block.tensor
            def _(pe):
                pe.matmul(ps[0:E, 0, 0:1], carry[:, T, :], ones[:, 0:1], start=True, stop=True).then_inc(counted, 1)
                pe.wait_ge(marked, 1)
                pe.matmul(ps[0:E, 1, 0:1], upper[0:E, 0:E], is_over, start=True, stop=True).then_inc(ranked, 1)
                pe.wait_ge(marked, 2)
                pe.wait_ge(numbered, 1)
                pe.matmul(ps[0:1, 2, 0:E], number[0:E, 0:1], marks, start=True, stop=True)
                pe.matmul(ps[0:1, 2, E:E + 1], ones[0:E, 0:1], is_over, start=True, stop=True).then_inc(listed, 1)

            @block.vector
            def _(dve):
                dve.wait_ge(counted, 1)
                dve.tensor_scalar(is_over, ps[0:E, 0, 0:1], 2.0 * P + 0.5, None, ALU.is_gt)
                dve.drain().then_inc(marked, 1)
                dve.wait_ge(ranked, 1)
                dve.tensor_copy(rank, ps[0:E, 1, 0:1])
                dve.drain()
                dve.wait_ge(numbered, 1)
                dve.tensor_scalar(marks, place[0:E, :], rank, is_over, ALU.is_equal, ALU.mult)
                dve.drain().then_inc(marked, 1)
                dve.wait_ge(listed, 1)
                dve.tensor_copy(over[0:1, :], ps[0:1, 2, 0:E + 1])


class Item:

    def __init__(self, pair, q, items):
        self.pair, self.q, self.items = pair, q, items

    def __add__(self, n):
        return Item(self.pair, self.q + n, self.items)

    def __sub__(self, n):
        return self + -n

    @property
    def e(self):
        return self.pair * 2 + self.q

    @property
    def parity(self):
        return self.q % 2

    @property
    def turn(self):
        return self.pair + self.q // 2

    @property
    def exists(self):
        return not isinstance(self.pair, int) or 0 <= self.e < self.items


class NetworkBuffers:

    def __init__(self, nc, ctx):
        def sb(name, shape, dt=F32):
            return ctx.enter_context(nc.sbuf_tensor(name, shape, dt))

        nb = 2
        self.ps = ctx.enter_context(nc.psum_tensor("ps_c", [P, 8, 512], F32))
        self.raw_gu = sb("raw_gu", [P, 2, 2, DC * F])
        self.raw_d = sb("raw_d", [P, 2, NF, D])
        self.gu_hi, self.gu_lo = (sb(n, [P, 2, 2, DC, F], F32R) for n in ("gu_hi", "gu_lo"))
        self.d_hi, self.d_lo = (sb(n, [P, 2, NF, D], F32R) for n in ("d_hi", "d_lo"))
        self.xg = sb("xg", [P, 2, nb, D])
        self.xt_hi, self.xt_lo = (sb(n, [P, 2, DC, nb * P], F32R) for n in ("xt_hi", "xt_lo"))
        self.sg, self.h = sb("sg", [P, 2, nb * P]), sb("h", [P, 2, nb * P])
        self.h_hi, self.h_lo = (sb(n, [P, 2, NF, nb * P], F32R) for n in ("h_hi", "h_lo"))
        self.y = sb("y", [P, 2, nb, D])
        self.ids_g, self.ids_s = sb("ids_g", [P, 2, nb], I32), sb("ids_s", [P, 2, nb], I32)
        self.wsl = sb("wsl", [P, 2, nb])
        self.ident = sb("ident_c", [P, P])
        self.slots = sb("slots", [P, E * CB, 2])
        self.ids = sb("ids", [P, E * CB], I32)
        self.w = sb("w", [P, E * CB])
        self.sh_ids = sb("sh_ids", [P, SHARED * (N // (2 * P)) * 2], I32)
        self.sh_w = sb("sh_w", [P, SHARED * (N // (2 * P)) * 2])


def network_section(nc, ctx, B, name, items, wide, ids, weights, w_gu, w_d, weight_of, hbuf, out):
    nb = 2
    W = nb * P
    ps = B.ps
    sets = 3
    XT0, GU0, Y0 = 0, 2, 5

    def sem(what):
        return ctx.enter_context(nc.semaphore(f"{name}_{what}"))

    def sig(what, per):
        return Signal(sem(what), per)

    def pair_of(what, per):
        return [Signal(sem(f"{what}{p}"), per) for p in range(2)]

    gu_in, d_in = pair_of("gu_in", 16), pair_of("d_in", 32)
    rows_in = pair_of("rows_in", 16 * nb)
    added = sig("added", 16 * nb)
    gu_hi, gu_lo = sig("gu_hi", 2), sig("gu_lo", 2)
    d_hi, d_lo = sig("d_hi", 1), sig("d_lo", 1)
    xt_ready = sig("xt_ready", DC)
    xt_hi, xt_lo = sig("xt_hi", DC), sig("xt_lo", DC)
    gu_ready = sig("gu_ready", NF)
    sg_ready = sig("sg_ready", NF)
    h_ready = sig("h_ready", NF)
    h_hi, h_lo = sig("h_hi", NF), sig("h_lo", NF)
    w_ready = sig("w_ready", 1)
    y_ready = sig("y_ready", nb)
    y_taken = sig("y_taken", nb)
    g_copied, s_copied = sig("g_copied", 1), sig("s_copied", 1)
    passed = sem("passed")

    def drive(eng, before, slot, after):
        before(Item(0, 0, items))
        for q in range(2):
            slot(Item(0, q, items))
        with eng.Fori(1, items // 2 - 1) as pair:
            for q in range(2):
                slot(Item(pair, q, items))
        for q in range(2):
            slot(Item(items // 2 - 1, q, items))
        after(Item(items // 2 - 1, 1, items))

    none = lambda item: None

    def gu_banks(c, m):
        bank = ps[0:m, GU0 + c % sets]
        return bank[:, 0:W], bank[:, W:2 * W]

    def chunk(item, c, back):
        n = c - back
        return item + n // NF, n % NF

    def sync_program(sp):
        def load(it):
            p = it.parity
            if (it - 2).exists:
                sp.wait_ge(gu_lo.sem, gu_lo.value((it - 2).e, 2))
            sp.dma_start(B.raw_gu[:, p].rearrange("p a n -> p (a n)"), w_gu(weight_of(it))).then_inc(gu_in[p].sem, 16)
            if (it - 2).exists:
                sp.wait_ge(d_lo.sem, d_lo.value((it - 2).e, 1))
            src = w_d(weight_of(it))
            sp.dma_start(B.raw_d[:, p, 0:2, :], src[0:2 * P, :].rearrange("(c p) n -> p c n", p=P)).then_inc(d_in[p].sem, 16)
            sp.dma_start(B.raw_d[0:FCH[2][1], p, 2, :], src[2 * P:F, :]).then_inc(d_in[p].sem, 16)
        drive(sp, none, load, none)

    def gather(pool, it):
        if not it.exists:
            return
        p = it.parity
        if (it - 2).exists:
            pool.wait_ge(rows_in[p].sem, rows_in[p].value((it - 2).turn, 16 * nb))
        pool.tensor_copy(B.ids_g[:, p, 0:nb], ids[:, bass.ds(it.e * wide, nb)]).then_inc(g_copied.sem, 1)
        if (it - 2).exists:
            pool.wait_ge(xt_ready.sem, xt_ready.value((it - 2).e, DC))
        pool.wait_ge(g_copied.sem, g_copied.value(it.e, 1))
        pool.sem_inc(passed, 1)
        for k in range(nb):
            pool.indirect_dma_start(
                out=B.xg[:, p, k, :], out_offset=None, in_=hbuf,
                in_offset=bass.IndirectOffsetOnAxis(B.ids_g[:, p, k:k + 1], 0),
                bounds_check=N - 1, oob_is_err=False).then_inc(rows_in[p].sem, 16)

    def scatter(pool, it):
        if not it.exists:
            return
        p = it.parity
        if (it - 1).exists:
            pool.wait_ge(added.sem, added.value((it - 1).e, 16 * nb))
        pool.tensor_copy(B.ids_s[:, p, 0:nb], ids[:, bass.ds(it.e * wide, nb)]).then_inc(s_copied.sem, 1)
        pool.wait_ge(y_taken.sem, y_taken.value(it.e, nb))
        pool.wait_ge(s_copied.sem, s_copied.value(it.e, 1))
        pool.sem_inc(passed, 1)
        for k in range(nb):
            pool.indirect_dma_start(
                out=out, out_offset=bass.IndirectOffsetOnAxis(B.ids_s[:, p, k:k + 1], 0),
                in_=B.y[:, p, k, :], in_offset=None, bounds_check=N - 1, oob_is_err=False,
                compute_op=ALU.add).then_inc(added.sem, 16)

    def pool_program(pool):
        def before(it):
            gather(pool, it)
            gather(pool, it + 1)

        def slot(it):
            gather(pool, it + 2)
            scatter(pool, it - 1)

        def after(it):
            scatter(pool, it)
            pool.wait_ge(added.sem, added.value(it.e, 16 * nb))

        drive(pool, before, slot, after)

    HALVES = [(0, 0), (1, 1)]

    def cut_gu(eng, it, half, act):
        if not it.exists:
            return
        p = it.parity
        hi, raw = B.gu_hi[:, p, half], B.raw_gu[:, p, half].rearrange("p (c f) -> p c f", c=DC)
        if act:
            eng.wait_ge(gu_in[p].sem, gu_in[p].value(it.turn, 16))
            if (it - 2).exists:
                eng.wait_ge(gu_ready.sem, gu_ready.value((it - 2).e, NF))
            eng.activation(hi, raw, ACT.Copy).then_inc(gu_hi.sem, 1)
        else:
            eng.wait_ge(gu_hi.sem, gu_hi.value(it.e, half + 1))
            eng.tensor_tensor(B.gu_lo[:, p, half], raw, hi.bitcast(F32), ALU.subtract).then_inc(gu_lo.sem, 1)

    def cut_d(eng, it, act):
        p = it.parity
        if act:
            eng.wait_ge(d_in[p].sem, d_in[p].value(it.turn, 32))
            if (it - 2).exists:
                eng.wait_ge(y_ready.sem, y_ready.value((it - 2).e, nb))
            eng.activation(B.d_hi[:, p, 0:2], B.raw_d[:, p, 0:2], ACT.Copy)
            eng.activation(B.d_hi[0:96, p, 2], B.raw_d[0:96, p, 2], ACT.Copy).then_inc(d_hi.sem, 1)
        else:
            eng.wait_ge(d_hi.sem, d_hi.value(it.e, 1))
            eng.tensor_tensor(B.d_lo[:, p, 0:2], B.raw_d[:, p, 0:2], B.d_hi[:, p, 0:2].bitcast(F32), ALU.subtract)
            eng.tensor_tensor(B.d_lo[0:96, p, 2], B.raw_d[0:96, p, 2], B.d_hi[0:96, p, 2].bitcast(F32), ALU.subtract).then_inc(d_lo.sem, 1)

    def cut_x(eng, it, c, act):
        if not it.exists:
            return
        p = it.parity
        src = ps[:, XT0 + c % 2, 0:W]
        if act:
            eng.wait_ge(xt_ready.sem, xt_ready.value(it.e, c + 1))
            if c == 0 and (it - 2).exists:
                eng.wait_ge(gu_ready.sem, gu_ready.value((it - 2).e, NF))
            eng.activation(B.xt_hi[:, p, c, 0:W], src, ACT.Copy).then_inc(xt_hi.sem, 1)
        else:
            eng.wait_ge(xt_hi.sem, xt_hi.value(it.e, c + 1))
            eng.tensor_tensor(B.xt_lo[:, p, c, 0:W], src, B.xt_hi[:, p, c, 0:W].bitcast(F32), ALU.subtract).then_inc(xt_lo.sem, 1)

    def scalar_program(act):
        def before(it):
            cut_gu(act, it, 0, True)
            cut_gu(act, it, 1, True)
            for c in range(DC):
                cut_x(act, it, c, True)

        def silu(it, c):
            m = FCH[c][1]
            act.wait_ge(gu_ready.sem, gu_ready.value(it.e, c + 1))
            j, n = chunk(it, c, 2)
            if j.exists:
                act.wait_ge(h_ready.sem, h_ready.value(j.e, n + 1))
            act.activation(B.sg[0:m, (it.parity * NF + c) % 2, 0:W], gu_banks(c, m)[0], ACT.Silu).then_inc(sg_ready.sem, 1)

        def high(it, c):
            m = FCH[c][1]
            act.wait_ge(h_ready.sem, h_ready.value(it.e, c + 1))
            if c == 0 and (it - 2).exists:
                act.wait_ge(y_ready.sem, y_ready.value((it - 2).e, nb))
            act.activation(B.h_hi[0:m, it.parity, c, 0:W], B.h[0:m, (it.parity * NF + c) % 2, 0:W], ACT.Copy).then_inc(h_hi.sem, 1)

        def slot(it):
            cut_gu(act, it + 1, 0, True)
            silu(it, 0)
            cut_x(act, it + 1, 0, True)
            cut_x(act, it + 1, 1, True)
            high(it, 0)
            cut_gu(act, it + 1, 1, True)
            silu(it, 1)
            cut_x(act, it + 1, 2, True)
            cut_x(act, it + 1, 3, True)
            high(it, 1)
            cut_d(act, it, True)
            silu(it, 2)
            high(it, 2)
            results(it - 1)

        def results(it):
            if not it.exists:
                return
            act.wait_ge(w_ready.sem, w_ready.value(it.e, 1))
            if (it - 2).exists:
                act.wait_ge(added.sem, added.value((it - 2).e, 16 * nb))
            for k in range(nb):
                act.wait_ge(y_ready.sem, y_ready.value(it.e, k + 1))
                act.activation(B.y[:, it.parity, k, :], ps[:, Y0 + k % 2, :], ACT.Copy,
                                          scale=B.wsl[:, it.parity, k:k + 1]).then_inc(y_taken.sem, 1)

        drive(act, before, slot, results)

    def vector_program(dve):
        def before(it):
            cut_gu(dve, it, 0, False)
            cut_gu(dve, it, 1, False)
            for c in range(DC):
                cut_x(dve, it, c, False)

        def mix(it, c):
            m = FCH[c][1]
            dve.wait_ge(sg_ready.sem, sg_ready.value(it.e, c + 1))
            j, n = chunk(it, c, 2)
            if j.exists:
                dve.wait_ge(h_hi.sem, h_hi.value(j.e, n + 1))
            b = (it.parity * NF + c) % 2
            dve.tensor_tensor(B.h[0:m, b, 0:W], B.sg[0:m, b, 0:W], gu_banks(c, m)[1], ALU.mult).then_inc(h_ready.sem, 1)

        def rest(it, c):
            m = FCH[c][1]
            dve.wait_ge(h_hi.sem, h_hi.value(it.e, c + 1))
            dve.tensor_tensor(B.h_lo[0:m, it.parity, c, 0:W], B.h[0:m, (it.parity * NF + c) % 2, 0:W],
                                      B.h_hi[0:m, it.parity, c, 0:W].bitcast(F32), ALU.subtract).then_inc(h_lo.sem, 1)

        def slot(it):
            if (it - 2).exists:
                dve.wait_ge(y_taken.sem, y_taken.value((it - 2).e, nb))
            dve.tensor_copy(B.wsl[:, it.parity, 0:nb], weights[:, bass.ds(it.e * wide, nb)]).then_inc(w_ready.sem, 1)
            cut_gu(dve, it + 1, 0, False)
            mix(it, 0)
            cut_x(dve, it + 1, 0, False)
            cut_x(dve, it + 1, 1, False)
            rest(it, 0)
            cut_gu(dve, it + 1, 1, False)
            mix(it, 1)
            cut_x(dve, it + 1, 2, False)
            cut_x(dve, it + 1, 3, False)
            rest(it, 1)
            cut_d(dve, it, False)
            mix(it, 2)
            rest(it, 2)

        drive(dve, before, slot, none)

    def tensor_program(pe):
        def transpose_chunk(it, c):
            if not it.exists:
                return
            if c == 0:
                pe.wait_ge(rows_in[it.parity].sem, rows_in[it.parity].value(it.turn, 16 * nb))
            j, n = (it, c - 2) if c >= 2 else (it - 1, c + 2)
            if j.exists:
                pe.wait_ge(xt_lo.sem, xt_lo.value(j.e, n + 1))
            for k in range(nb):
                last = pe.transpose(ps[:, XT0 + c % 2, k * P:(k + 1) * P],
                                    B.xg[:, it.parity, k, c * P:(c + 1) * P], B.ident[:])
            last.then_inc(xt_ready.sem, 1)

        def gate_up(it, c):
            o, m = FCH[c]
            p = it.parity
            if c == 0:
                pe.wait_ge(gu_lo.sem, gu_lo.value(it.e, 2))
                pe.wait_ge(xt_lo.sem, xt_lo.value(it.e, DC))
            j, n = chunk(it, c, sets)
            if j.exists:
                pe.wait_ge(h_ready.sem, h_ready.value(j.e, n + 1))
            for half in range(2):
                steps = [(w, x, d) for w, x in ((B.gu_hi, B.xt_hi), (B.gu_hi, B.xt_lo), (B.gu_lo, B.xt_hi))
                         for d in range(DC)]
                for i, (w, x, d) in enumerate(steps):
                    last = pe.matmul(gu_banks(c, m)[half], w[:, p, half, d, o:o + m], x[:, p, d, 0:W],
                                     start=i == 0, stop=i == len(steps) - 1)
            last.then_inc(gu_ready.sem, 1)

        def down(it):
            if not it.exists:
                return
            p = it.parity
            pe.wait_ge(d_lo.sem, d_lo.value(it.e, 1))
            pe.wait_ge(h_lo.sem, h_lo.value(it.e, NF))
            for k in range(nb):
                if (it - 1).exists:
                    pe.wait_ge(y_taken.sem, y_taken.value((it - 1).e, k + 1))
                steps = [(h, w, c) for h, w in ((B.h_hi, B.d_hi), (B.h_hi, B.d_lo), (B.h_lo, B.d_hi))
                         for c in range(NF)]
                for i, (h, w, c) in enumerate(steps):
                    m = FCH[c][1]
                    last = pe.matmul(ps[:, Y0 + k % 2, :], h[0:m, p, c, k * P:(k + 1) * P], w[0:m, p, c, :],
                                     start=i == 0, stop=i == len(steps) - 1)
                last.then_inc(y_ready.sem, 1)

        def before(it):
            for c in range(DC):
                transpose_chunk(it, c)

        def slot(it):
            gate_up(it, 0)
            transpose_chunk(it + 1, 0)
            transpose_chunk(it + 1, 1)
            gate_up(it, 1)
            transpose_chunk(it + 1, 2)
            transpose_chunk(it + 1, 3)
            gate_up(it, 2)
            down(it - 1)

        drive(pe, before, slot, down)

    return dict(sync=sync_program, gpsimd=pool_program, scalar=scalar_program,
                vector=vector_program, tensor=tensor_program)


def third_blocks(nc, ctx, B, over, w_gu, w_d, hbuf, out):
    ps = B.ps
    XT, GU0, Y0 = 0, 1, 4
    p = 0

    def sig(what, per, first=0):
        return Signal(ctx.enter_context(nc.semaphore(f"third_{what}")), per, first)

    w_in = sig("w_in", 48)
    w_cut = sig("w_cut", 1, first=1)
    ids_copied = sig("ids_copied", 1)
    rows_in = sig("rows_in", 16)
    added = sig("added", 16)
    xt_ready, xt_hi, xt_lo = sig("xt_ready", 1), sig("xt_hi", 1), sig("xt_lo", 1)
    w_hi = sig("w_hi", 3)
    gu_lo = sig("gu_lo", 2)
    gu_ready, sg_ready = sig("gu_ready", NF), sig("sg_ready", NF)
    h_ready, h_hi, h_lo = sig("h_ready", NF), sig("h_hi", NF), sig("h_lo", NF)
    y_ready, y_taken = sig("y_ready", 1), sig("y_taken", 1)
    passed = ctx.enter_context(nc.semaphore("third_passed"))
    xt = [t[:, p, :, 0:P] for t in (B.xt_hi, B.xt_lo)]
    xt_bank = ps[:, XT, :].rearrange("p (c n) -> p c n", c=DC)
    gate = [ps[0:m, GU0 + c, 0:P] for c, (_, m) in enumerate(FCH)]
    up = [ps[0:m, GU0 + c, P:2 * P] for c, (_, m) in enumerate(FCH)]
    sg, h = ([t[0:m, c % 2, (c // 2) * P:(c // 2 + 1) * P] for c, (_, m) in enumerate(FCH)] for t in (B.sg, B.h))
    hh, hl = ([t[0:m, p, c, 0:P] for c, (_, m) in enumerate(FCH)] for t in (B.h_hi, B.h_lo))
    D_PARTS = [(slice(0, P), slice(0, 2)), (slice(0, FCH[2][1]), slice(2, 3))]

    def each(eng, body):
        LONG = N * TOPK // (2 * P + 1)
        many = eng.value_load(over[0:1, E:E + 1], min_val=0, max_val=E)
        with eng.Fori(0, LONG) as j:
            with eng.If(many > j):
                body(j)

    def expert(eng, j):
        return eng.value_load(over[0:1, bass.ds(j, 1)], min_val=0, max_val=E - 1)

    def sync(sp):
        sp.sem_inc(w_cut.sem, 1)

        def body(j):
            e = expert(sp, j)
            sp.wait_ge(w_cut.sem, w_cut.value(j, 0))
            sp.dma_start(B.raw_gu[:, p].rearrange("p a n -> p (a n)"), w_gu(e)).then_inc(w_in.sem, 16)
            src = w_d(e)
            sp.dma_start(B.raw_d[:, p, 0:2, :], src[0:2 * P, :].rearrange("(c p) n -> p c n", p=P)).then_inc(w_in.sem, 16)
            sp.dma_start(B.raw_d[0:FCH[2][1], p, 2, :], src[2 * P:F, :]).then_inc(w_in.sem, 16)
        each(sp, body)

    def gpsimd(pool):
        def body(j):
            e = expert(pool, j)
            pool.tensor_copy(B.wsl[:, p, 0:1], B.w[:, bass.ds(e * CB + 2, 1)])
            pool.tensor_copy(B.ids_g[:, p, 0:1], B.ids[:, bass.ds(e * CB + 2, 1)]).then_inc(ids_copied.sem, 1)
            pool.wait_ge(ids_copied.sem, ids_copied.value(j, 1))
            pool.sem_inc(passed, 1)
            pool.indirect_dma_start(
                out=B.xg[:, p, 0, :], out_offset=None, in_=hbuf,
                in_offset=bass.IndirectOffsetOnAxis(B.ids_g[:, p, 0:1], 0),
                bounds_check=N - 1, oob_is_err=False).then_inc(rows_in.sem, 16)
            pool.wait_ge(y_taken.sem, y_taken.value(j, 1))
            pool.sem_inc(passed, 1)
            pool.indirect_dma_start(
                out=out, out_offset=bass.IndirectOffsetOnAxis(B.ids_g[:, p, 0:1], 0),
                in_=B.y[:, p, 0, :], in_offset=None, bounds_check=N - 1, oob_is_err=False,
                compute_op=ALU.add).then_inc(added.sem, 16)
            pool.wait_ge(added.sem, added.value(j, 16))
            pool.sem_inc(passed, 1)
        each(pool, body)

    def scalar(act):
        def body(j):
            act.wait_ge(w_in.sem, w_in.value(j, 48))
            for half in range(2):
                raw = B.raw_gu[:, p, half].rearrange("p (c f) -> p c f", c=DC)
                act.activation(B.gu_hi[:, p, half], raw, ACT.Copy).then_inc(w_hi.sem, 1)
            act.wait_ge(xt_ready.sem, xt_ready.value(j, 1))
            act.activation(xt[0], xt_bank, ACT.Copy).then_inc(xt_hi.sem, 1)
            act.activation(B.d_hi[0:P, p, 0:2], B.raw_d[0:P, p, 0:2], ACT.Copy)
            act.activation(B.d_hi[0:96, p, 2], B.raw_d[0:96, p, 2], ACT.Copy).then_inc(w_hi.sem, 1)
            for c in range(NF):
                act.wait_ge(gu_ready.sem, gu_ready.value(j, c + 1))
                act.activation(sg[c], gate[c], ACT.Silu).then_inc(sg_ready.sem, 1)
                act.wait_ge(h_ready.sem, h_ready.value(j, c + 1))
                act.activation(hh[c], h[c], ACT.Copy).then_inc(h_hi.sem, 1)
            act.wait_ge(y_ready.sem, y_ready.value(j, 1))
            act.activation(B.y[:, p, 0, :], ps[:, Y0, :], ACT.Copy, scale=B.wsl[:, p, 0:1]).then_inc(y_taken.sem, 1)
        each(act, body)

    def vector(dve):
        def body(j):
            for half in range(2):
                raw = B.raw_gu[:, p, half].rearrange("p (c f) -> p c f", c=DC)
                dve.wait_ge(w_hi.sem, w_hi.value(j, half + 1))
                dve.tensor_tensor(B.gu_lo[:, p, half], raw, B.gu_hi[:, p, half].bitcast(F32),
                                  ALU.subtract).then_inc(gu_lo.sem, 1)
            dve.wait_ge(xt_hi.sem, xt_hi.value(j, 1))
            dve.tensor_tensor(xt[1], xt_bank, xt[0].bitcast(F32), ALU.subtract).then_inc(xt_lo.sem, 1)
            dve.wait_ge(w_hi.sem, w_hi.value(j, 3))
            dve.tensor_tensor(B.d_lo[:, p, 0:2], B.raw_d[:, p, 0:2], B.d_hi[:, p, 0:2].bitcast(F32), ALU.subtract)
            dve.tensor_tensor(B.d_lo[0:96, p, 2], B.raw_d[0:96, p, 2], B.d_hi[0:96, p, 2].bitcast(F32),
                              ALU.subtract).then_inc(w_cut.sem, 1)
            for c in range(NF):
                dve.wait_ge(sg_ready.sem, sg_ready.value(j, c + 1))
                dve.tensor_tensor(h[c], sg[c], up[c], ALU.mult).then_inc(h_ready.sem, 1)
                dve.wait_ge(h_hi.sem, h_hi.value(j, c + 1))
                dve.tensor_tensor(hl[c], h[c], hh[c].bitcast(F32), ALU.subtract).then_inc(h_lo.sem, 1)
        each(dve, body)

    def tensor(pe):
        def body(j):
            pe.wait_ge(rows_in.sem, rows_in.value(j, 16))
            for c in range(DC):
                last = pe.transpose(ps[:, XT, c * P:(c + 1) * P], B.xg[:, p, 0, c * P:(c + 1) * P], B.ident[:])
            last.then_inc(xt_ready.sem, 1)
            pe.wait_ge(gu_lo.sem, gu_lo.value(j, 2))
            pe.wait_ge(xt_lo.sem, xt_lo.value(j, 1))
            for c, (o, m) in enumerate(FCH):
                for half, dst in enumerate((gate[c], up[c])):
                    steps = [(w, x, d) for w, x in ((B.gu_hi, xt[0]), (B.gu_hi, xt[1]), (B.gu_lo, xt[0]))
                             for d in range(DC)]
                    for i, (w, x, d) in enumerate(steps):
                        last = pe.matmul(dst, w[:, p, half, d, o:o + m], x[:, d, :],
                                         start=i == 0, stop=i == len(steps) - 1)
                last.then_inc(gu_ready.sem, 1)
            pe.wait_ge(w_cut.sem, w_cut.value(j, 1))
            pe.wait_ge(h_lo.sem, h_lo.value(j, NF))
            steps = [(a, w, c) for a, w in ((hh, B.d_hi), (hh, B.d_lo), (hl, B.d_hi)) for c in range(NF)]
            for i, (a, w, c) in enumerate(steps):
                last = pe.matmul(ps[:, Y0, :], a[c], w[0:FCH[c][1], p, c, :], start=i == 0, stop=i == len(steps) - 1)
            last.then_inc(y_ready.sem, 1)
        each(pe, body)

    return dict(sync=sync, gpsimd=gpsimd, scalar=scalar, vector=vector, tensor=tensor)


def network_phase(nc, ins, out, hbuf, table, over):
    outer = ExitStack()
    with outer as ctx:
        B = NetworkBuffers(nc, ctx)
        outf = out.rearrange("b s n -> (b s) n")
        tab_loaded, made = (ctx.enter_context(nc.semaphore(n)) for n in ("tab_loaded", "made"))
        blocks = N // (2 * P)
        with nc.Block() as block:
            @block.sync
            def _(sp):
                sp.dma_start(B.slots[:].rearrange("p n c -> p (n c)"),
                             table.rearrange("(p n) c -> p (n c)", p=P)).then_inc(tab_loaded, 16)

            @block.gpsimd
            def _(pool):
                pool.memset(B.ident[:], 0.0)
                pool.memset(B.xg[:], 0.0)
                pool.memset(B.sh_w[:], 1.0)
                pool.iota(B.sh_ids[:], [[0, SHARED], [P, 2 * blocks]], base=0, channel_multiplier=1)
                pool.drain()
                pool.affine_select(out=B.ident[:], in_=B.ident[:], compare_op=ALU.not_equal, fill=1.0,
                                   base=0, pattern=[[-1, P]], channel_multiplier=1)

            @block.vector
            def _(dve):
                dve.wait_ge(tab_loaded, 16)
                dve.tensor_copy(B.ids[:], B.slots[:, :, 0])
                dve.tensor_copy(B.w[:], B.slots[:, :, 1])

        shared = network_section(
            nc, ctx, B, "shared", SHARED * blocks, 2, B.sh_ids, B.sh_w,
            lambda e: ins["sh_gu"][bass.ds(e, 1)].rearrange("a p n -> p (a n)"),
            lambda e: ins["sh_d"][bass.ds(e, 1)].rearrange("a f n -> (a f) n"),
            lambda it: it.e // blocks, hbuf, outf)
        expert_gu = lambda e: ins["w_gu"][bass.ds(e, 1)].rearrange("a p n -> p (a n)")
        expert_d = lambda e: ins["w_d"][bass.ds(e, 1)].rearrange("a f n -> (a f) n")
        experts = network_section(nc, ctx, B, "expert", E, CB, B.ids, B.w, expert_gu, expert_d,
                                  lambda it: it.e, hbuf, outf)
        thirds = third_blocks(nc, ctx, B, over, expert_gu, expert_d, hbuf, outf)

        for sections in ((shared,), (experts,), (thirds,)):
            with nc.Block() as block:
                @block.sync
                def _(sp):
                    for section in sections:
                        section["sync"](sp)

                @block.gpsimd
                def _(pool):
                    for section in sections:
                        section["gpsimd"](pool)

                @block.scalar
                def _(act):
                    for section in sections:
                        section["scalar"](act)

                @block.vector
                def _(dve):
                    for section in sections:
                        section["vector"](dve)

                @block.tensor
                def _(pe):
                    for section in sections:
                        section["tensor"](pe)


def program(nc, ins, out):
    with ExitStack() as ctx:
        over = ctx.enter_context(nc.sbuf_tensor("over", [P, E + 1], I32))
        hbuf = nc.dram_tensor("h2_rows", [N, D], F32, kind="Internal").ap()
        table = nc.dram_tensor("slot_table", [E * CAP, 2], F32, kind="Internal").ap()
        kvd = nc.dram_tensor("kv_dca", [NB * DCA, 2 * D], F32, kind="Internal").ap()
        attention_phase(nc, ins, out, hbuf, table, kvd, over)
        network_phase(nc, ins, out, hbuf, table, over)


def kernel(x, ctx_1024, L0_xattn_Wq, L0_xattn_bq, L0_xattn_Wk, L0_xattn_bk, L0_xattn_Wv, L0_xattn_bv,
           L0_xattn_Wkv_dca, L0_xattn_bkv_dca, L0_xattn_qn_w, L0_xattn_qn_b, L0_xattn_kn_w, L0_xattn_kn_b,
           L0_xattn_kn_dca_w, L0_xattn_kn_dca_b, L0_xattn_Wo, L0_xattn_bo, L0_ffn_gate_w, L0_ffn_w_gate,
           L0_ffn_w_up, L0_ffn_w_down, L0_ffn_sh_gate, L0_ffn_sh_up, L0_ffn_sh_down):
    import numpy as np
    from concourse import bacc
    from concourse.bass_utils import run_bass_kernel_spmd

    c = np.ascontiguousarray
    kv = np.concatenate([L0_xattn_Wk, L0_xattn_Wv], 1).reshape(DY, H, 2, HD)
    kvb = np.concatenate([L0_xattn_bk, L0_xattn_bv]).reshape(H, 2, HD)
    ctx_t = np.asarray(ctx_1024).transpose(0, 2, 1)

    def gate_up(gate, up):
        w = np.stack([gate, up], 1).reshape(-1, 2, F, DC, P)
        return c(w.transpose(0, 4, 1, 3, 2).reshape(-1, P, 2 * DC * F))

    arrays = dict(
        x=c(x), ctxT=c(ctx_t), ctx_dcaT=c(ctx_t[:, :, MAIN:].transpose(1, 0, 2).reshape(DY, NB * DCA)),
        Wq=c(L0_xattn_Wq), bq=c(L0_xattn_bq), Wk=c(kv[:, :, 0].reshape(DY, D)), bk=c(kvb[:, 0].reshape(D)),
        Wv=c(kv[:, :, 1].reshape(DY, D)), bv=c(kvb[:, 1].reshape(D)), Wkv_dca=c(L0_xattn_Wkv_dca),
        bkv_dca=c(L0_xattn_bkv_dca), qn_w=c(L0_xattn_qn_w), qn_b=c(L0_xattn_qn_b), kn_w=c(L0_xattn_kn_w),
        kn_b=c(L0_xattn_kn_b), kn_dca_w=c(L0_xattn_kn_dca_w), kn_dca_b=c(L0_xattn_kn_dca_b),
        Wo=c(L0_xattn_Wo), bo=c(L0_xattn_bo), gate_wT=c(np.asarray(L0_ffn_gate_w).T),
        w_gu=gate_up(np.asarray(L0_ffn_w_gate), np.asarray(L0_ffn_w_up)),
        w_d=c(np.asarray(L0_ffn_w_down).transpose(0, 2, 1)),
        sh_gu=gate_up(np.asarray(L0_ffn_sh_gate).reshape(SHARED, F, D), np.asarray(L0_ffn_sh_up).reshape(SHARED, F, D)),
        sh_d=c(np.asarray(L0_ffn_sh_down).T.reshape(SHARED, F, D)))
    nc = bacc.Bacc("TRN2", target_bir_lowering=False, num_devices=1)
    ins = {k: nc.dram_tensor(f"in_{k}", a.shape, mybir.dt.from_np(a.dtype), kind="ExternalInput").ap()
           for k, a in arrays.items()}
    out = nc.dram_tensor("out_0", (NB, S, D), F32, kind="ExternalOutput").ap()
    program(nc, ins, out)
    r = run_bass_kernel_spmd(nc, [{f"in_{k}": a for k, a in arrays.items()}], core_ids=[0])
    return r.results[0]["out_0"]
```
